# Optimizing a Trainium2 kernel written in Bass

```python
import numpy as np
import jax
import jax.numpy as jnp

def _softmax(x, axis=-1):
    return jax.nn.softmax(x, axis=axis)

def _gelu(x):
    return jax.nn.gelu(x, approximate=True)

def _silu(x):
    return jax.nn.silu(x)

def _sigmoid(x):
    return jax.nn.sigmoid(x)

def _layernorm(x, axis=-1, eps=1e-05):
    m = jnp.mean(x, axis=axis, keepdims=True)
    v = jnp.var(x, axis=axis, keepdims=True)
    return (x - m) / jnp.sqrt(v + eps)

def _scatter_add(tgt, idx, src, axis=0):
    return tgt.at[idx].add(src)

def _segment_sum(src, seg, n):
    return jax.ops.segment_sum(src, seg, n)
kernel_name = 'mk_prb_d1_jaxref_r4_e89807'

def setup_inputs(seed: int=0):
    np.random.seed(seed)
    _w = jnp.asarray

    def _L0_attn_setup():
        import jax, jax.numpy as jnp
        import numpy as np
        B, T, D, H, R = (1, 1024, 256, 16, 64)
        HD = D // H
        STD = 0.02

        def _low_rank_proj(x, a, b):
            mid = jnp.einsum('btd,hdr->bhtr', x, a)
            return jnp.einsum('bhtr,hrd->bhtd', mid, b)
        key = jax.random.key(seed)
        ks = jax.random.split(key, 8)
        return {'hidden_states': jax.random.normal(ks[0], (B, T, D), jnp.float32), 'q_a': STD * jax.random.normal(ks[1], (H, D, R), jnp.float32), 'q_b': STD * jax.random.normal(ks[2], (H, R, HD), jnp.float32), 'k_a': STD * jax.random.normal(ks[3], (H, D, R), jnp.float32), 'k_b': STD * jax.random.normal(ks[4], (H, R, HD), jnp.float32), 'v_w': STD * jax.random.normal(ks[5], (D, D), jnp.float32), 'v_b': jnp.zeros((D,), jnp.float32), 'o_w': STD * jax.random.normal(ks[6], (D, D), jnp.float32), 'o_b': jnp.zeros((D,), jnp.float32)}
    _L0_attn_in = _L0_attn_setup()

    def _L0_ffn_setup():
        import jax, jax.numpy as jnp
        import numpy as np
        N_EXPERT_CAPACITY = 2
        key = jax.random.key(seed)
        k1, k2, k3, k4 = jax.random.split(key, 4)
        B, S, D, E, F = (8, 256, 256, 8, 512)
        x = jax.random.normal(k1, (B, S, D), dtype=jnp.float32)
        choice_w = jax.random.uniform(k2, (E, D), dtype=jnp.float32, minval=-1.0, maxval=1.0) * (1.0 / np.sqrt(D))
        w1 = jax.random.uniform(k3, (E, D, F), dtype=jnp.float32, minval=-1.0, maxval=1.0) * (1.0 / np.sqrt(D))
        w2 = jax.random.uniform(k4, (E, F, D), dtype=jnp.float32, minval=-1.0, maxval=1.0) * (1.0 / np.sqrt(F))
        return {'x': x, 'choice_w': choice_w, 'w1': w1, 'w2': w2}
    _L0_ffn_in = _L0_ffn_setup()
    _d = {'L0_attn_hidden_states': _L0_attn_in['hidden_states'], 'L0_attn_q_a': _L0_attn_in['q_a'], 'L0_attn_q_b': _L0_attn_in['q_b'], 'L0_attn_k_a': _L0_attn_in['k_a'], 'L0_attn_k_b': _L0_attn_in['k_b'], 'L0_attn_v_w': _L0_attn_in['v_w'], 'L0_attn_v_b': _L0_attn_in['v_b'], 'L0_attn_o_w': _L0_attn_in['o_w'], 'L0_attn_o_b': _L0_attn_in['o_b'], 'L0_ffn_choice_w': _L0_ffn_in['choice_w'], 'L0_ffn_w1': _L0_ffn_in['w1'], 'L0_ffn_w2': _L0_ffn_in['w2']}
    _x0 = _d['L0_attn_hidden_states']
    _d['L0_attn_hidden_states'] = jax.random.normal(jax.random.fold_in(jax.random.key(seed), 1), (16, 512, 256), dtype=_x0.dtype)
    del _x0
    return _d

def reference(L0_attn_hidden_states, L0_attn_q_a, L0_attn_q_b, L0_attn_k_a, L0_attn_k_b, L0_attn_v_w, L0_attn_v_b, L0_attn_o_w, L0_attn_o_b, L0_ffn_choice_w, L0_ffn_w1, L0_ffn_w2):

    def _L0_attn_ref(hidden_states, q_a, q_b, k_a, k_b, v_w, v_b, o_w, o_b):
        import jax, jax.numpy as jnp
        import numpy as np
        B, T, D, H, R = (1, 1024, 256, 16, 64)
        HD = D // H
        STD = 0.02

        def _low_rank_proj(x, a, b):
            mid = jnp.einsum('btd,hdr->bhtr', x, a)
            return jnp.einsum('bhtr,hrd->bhtd', mid, b)
        Bc, Tc, Dc = hidden_states.shape
        q = _low_rank_proj(hidden_states, q_a, q_b)
        k = _low_rank_proj(hidden_states, k_a, k_b)
        v = hidden_states @ v_w.T + v_b
        v = v.reshape(Bc, Tc, H, HD).transpose(0, 2, 1, 3)
        scale = 1.0 / np.sqrt(HD).astype(np.float32)
        att = jnp.einsum('bhtd,bhsd->bhts', q, k) * scale
        causal = jnp.tril(jnp.ones((Tc, Tc), dtype=bool))
        att = jnp.where(causal[None, None], att, jnp.finfo(att.dtype).min)
        att = jax.nn.softmax(att, axis=-1)
        y = jnp.einsum('bhts,bhsd->bhtd', att, v)
        y = y.transpose(0, 2, 1, 3).reshape(Bc, Tc, Dc)
        return y @ o_w.T + o_b

    def _L0_ffn_ref(x, choice_w, w1, w2):
        import jax, jax.numpy as jnp
        import numpy as np
        N_EXPERT_CAPACITY = 2
        B, S, D = x.shape
        E = choice_w.shape[0]
        k = S * N_EXPERT_CAPACITY // E
        probs = jax.nn.softmax(jnp.einsum('bsd,ed->bse', x, choice_w), axis=-1)
        G, I = jax.lax.top_k(jnp.swapaxes(probs, -1, -2), k)
        x_in = jnp.take_along_axis(x[:, None, :, :], I[..., None], axis=2)
        h = jax.nn.silu(jnp.einsum('bekd,edf->bekf', x_in, w1))
        x_mlp = jnp.einsum('bekf,efd->bekd', h, w2)
        b_idx = jnp.arange(B)[:, None, None]
        out = jnp.zeros_like(x).at[b_idx, I].add(G[..., None] * x_mlp)
        return out
    x = L0_attn_hidden_states
    xn = _layernorm(x, axis=-1)
    x = x + _L0_attn_ref(xn, L0_attn_q_a, L0_attn_q_b, L0_attn_k_a, L0_attn_k_b, L0_attn_v_w, L0_attn_v_b, L0_attn_o_w, L0_attn_o_b) + _L0_ffn_ref(xn, L0_ffn_choice_w, L0_ffn_w1, L0_ffn_w2)
    return x

_drawn_inputs = setup_inputs


def setup_inputs(seed=0):
    import zlib

    import numpy as np

    out = dict(_drawn_inputs(seed))
    spreads = {'L0_attn_v_b': (0.0, 0.292), 'L0_attn_o_b': (0.0, 0.1)}
    factors = {'L0_attn_q_a': 8.0,
     'L0_attn_q_b': 8.0,
     'L0_attn_k_a': 8.0,
     'L0_attn_k_b': 8.0,
     'L0_attn_v_w': 4.8}
    for name, (base, spread) in spreads.items():
        noise = np.random.default_rng([zlib.crc32(name.encode()), seed]).standard_normal(out[name].shape)
        drawn = base * np.exp(spread * noise) if base else spread * noise
        out[name] = jnp.asarray(drawn.astype(out[name].dtype))
    for name, factor in factors.items():
        out[name] = (out[name] * factor).astype(out[name].dtype)
    return out
```

```python
import concourse.bass as bass
from concourse import mybir
from contextlib import ExitStack

B, T, D = 16, 512, 256
H, HD, R = 16, 16, 64
E, F = 8, 512
CAP = T * 2 // E
P = 128
TT, DT, FT = T // P, D // P, F // P
EPS = 1e-5
GH = 4
GB = H // GH
NG = B * GB
UN = 10
TERMS = ((0, 0), (0, 1), (1, 0), (0, 2), (2, 0), (1, 1))
KS = HD * len(TERMS)
SHIFT = 2
NEG = -1e30
GB4 = 4
EG = B // GB4
SCALE = 1.0 / HD ** 0.5


def unit_parts(t, transposed):
    pair, r = divmod(t, 5)
    a, b = 2 * pair, 2 * pair + 1
    parts = [[(a, 3)], [(a, 2), (a, 0)], [(a, 1), (b, 1)], [(b, 3)], [(b, 2), (b, 0)]][r]
    out, col = [], 0
    for h, i in parts:
        out.append((h, 3 - i if transposed else i, col, P * (i + 1)))
        col += P * (i + 1)
    return out


def slot_steps(b, g):
    G = GB * b + g
    put = {t: [] for t in range(UN)}
    for t, j in zip((2, 3, 4, 5), range(TT)):
        put[t].append(("pv", G, j))
    if G + 2 < NG:
        put[4].append(("maxt", G + 2, 0))
    if g == 0:
        if b + 2 < B:
            put[0].append(("xload", b + 2, 0))
            put[9].append(("lnstat", b + 2, 0))
        if b >= 1 and b + 1 < B:
            put[1].append(("mid", b + 1, 3))
        if b + 1 < B:
            for t, tt in zip((0, 8, 9), range(TT)):
                put[t].append(("v", b + 1, tt))
        if b >= 1:
            put[1].append(("yt", b - 1, 0))
            put[6].append(("yt", b - 1, 1))
    elif g == 1:
        if b + 1 < B:
            put[0].append(("v", b + 1, 3))
        if b >= 1:
            for t, tt in zip((1, 6, 8, 9), range(TT)):
                put[t].append(("o", b - 1, tt))
        if b + 2 < B:
            put[2].append(("lnstat", b + 2, 1))
            put[8].append(("lnapply", b + 2, 0))
    elif g == 2:
        put[1].append(("xres", b, 0))
        if b + 2 < B:
            put[0].append(("xt", b + 2, 0))
            put[1].append(("xt", b + 2, 1))
            put[6].append(("qk_first", b + 2, 0))
            put[8].append(("qk", b + 2, 0))
            put[9].append(("qk_first", b + 2, 1))
    elif g == 3 and b + 2 < B:
        put[0] += [("qk", b + 2, 1), ("mid", b + 2, 0)]
        put[1].append(("qk_first", b + 2, 2))
        put[2].append(("mid", b + 2, 1))
        put[6].append(("qk", b + 2, 2))
        put[8] += [("qk_first", b + 2, 3), ("mid", b + 2, 2)]
        put[9].append(("qk", b + 2, 3))
    put[7].append(("ytr", G, 0))
    out = []
    for t in range(UN):
        out += [("scoret", G + 1, t)] * (G + 1 < NG) + [("score", G + 3, t)] * (G + 3 < NG) + put[t]
    return out


def prologue_steps():
    out = [("xload", 0, 0), ("lnstat", 0, 0), ("lnstat", 0, 1), ("lnapply", 0, 0), ("xload", 1, 0)]
    for w in range(2):
        for dt in range(DT):
            out += [("foldt", 2 * w + dt, half) for half in range(2)] + [("fold", 2 * w + dt, 0)]
    out += [("wv", dt, 0) for dt in range(DT)]
    for b in range(2):
        if b == 1:
            out += [("lnstat", 1, 0), ("lnstat", 1, 1), ("lnapply", 1, 0)]
        out += [("xt", b, dt) for dt in range(DT)]
        for mt in range(4):
            out += [("qk_first", b, mt), ("qk", b, mt), ("mid", b, mt)]
        if b == 0:
            out += [("v", 0, tt) for tt in range(TT)]
            out += [("wo", dt, 0) for dt in range(DT)]
            out += [("score", 0, t) for t in range(UN)]
    out += [("score", 1, t) for t in range(UN)] + [("maxt", 0, 0)]
    out += [("score", 2, t) for t in range(UN)] + [("maxt", 1, 0)]
    return out + [("scoret", 0, t) for t in range(UN)]


def epilogue_steps():
    return [("yt", B - 1, 0), ("yt", B - 1, 1), *[("o", B - 1, tt) for tt in range(TT)]]


def pair_steps(i):
    return [s for b in (2 * i, 2 * i + 1) for g in range(GB) for s in slot_steps(b, g)]


def build(nc, x, q_a, q_b, k_a, k_b, v_w, v_b, o_w, o_b, choice_w, w1, w2, out):
    fp32, f32r, bf16 = mybir.dt.float32, mybir.dt.float32r, mybir.dt.bfloat16
    i32, u32 = mybir.dt.int32, mybir.dt.uint32
    ALU, ACT, AX = mybir.AluOpType, mybir.ActivationFunctionType, mybir.AxisListType

    PAIRS = B // 2
    every = prologue_steps() + [s for i in range(PAIRS) for s in pair_steps(i)] + epilogue_steps()
    shared = [s for s in every if s[0] in ("foldt", "fold", "wv", "wo", "xt", "qk", "v", "maxt", "ytr", "yt", "o")]
    unit_of = {s: n for n, s in enumerate(shared)}
    split_of = {s: n for n, s in enumerate(s for s in shared if s[0] in ("fold", "wv", "wo", "xt", "qk", "yt"))}
    U_PAIR, S_PAIR = 48, 16
    for i in range(1, PAIRS - 2):
        for s, z in zip(pair_steps(i), pair_steps(i + 1)):
            assert s not in unit_of or unit_of[z] - unit_of[s] == U_PAIR
            assert s not in split_of or split_of[z] - split_of[s] == S_PAIR

    x_v = x.rearrange("b (t p) d -> b p t d", p=P)
    out_v = out.rearrange("b (t p) d -> b p t d", p=P)
    out_rows = out.rearrange("b t d -> (b t) d")
    xn_dram = nc.dram_tensor("xn_rows", (B * T, D), fp32, kind="Internal").ap()
    xn_v = xn_dram.rearrange("(b t p) d -> b p t d", b=B, p=P)

    ctx = ExitStack()
    with ctx:
        def sem(name):
            return ctx.enter_context(nc.semaphore(name))

        def keep(name, shape, dt):
            return ctx.enter_context(nc.sbuf_tensor(name, shape, dt))

        ident = keep("ident", [P, P], fp32)
        ident_bf = keep("ident_bf", [P, P], bf16)
        logits = keep("logits", [P, TT, B, E], fp32)
        banks = [ctx.enter_context(nc.psum_tensor(f"bank{i}", [P, 512], fp32)) for i in range(8)]

        with ExitStack() as mem:
            def sb(name, shape, dt):
                return mem.enter_context(nc.sbuf_tensor(name, shape, dt))

            qstk = [sb(f"qstk{u}", [P, H, T], bf16) for u in range(2)]
            kstk = [sb(f"kstk{u}", [P, H, T], bf16) for u in range(2)]
            vaug = [sb(f"vaug{u}", [P, TT, H, 2 * HD], fp32) for u in range(2)]
            probs = [sb(f"probs{u}", [P, 2 * 5 * 512], fp32) for u in range(2)]
            xln = sb("xln", [P, TT, D], fp32)
            xn = sb("xn", [P, TT, D], fp32)
            xres = sb("xres", [P, TT, D], fp32)
            xt_hi = sb("xt_hi", [P, DT, T], f32r)
            xt_lo = sb("xt_lo", [P, DT, T], f32r)
            rest = [sb(f"rest{u}", [P, T], fp32) for u in range(2)]
            qk_part = [sb(f"qk_part{n}", [P, 4, T], bf16) for n in range(3)]
            yraw = [sb(f"yraw{u}", [P, T], fp32) for u in range(2)]
            ytok = sb("ytok", [P, TT, D], fp32)
            yt_hi = sb("yt_hi", [P, DT, T], f32r)
            yt_lo = sb("yt_lo", [P, DT, T], f32r)
            junk = [sb(f"junk{u}", [P, 512], bf16) for u in range(2)]
            maxrow = [sb(f"maxrow{u}", [2 * GH, T], bf16) for u in range(2)]
            rowmax = [sb(f"rowmax{u}", [P, TT, GH], fp32) for u in range(2)]
            negmax = [sb(f"negmax{u}", [P, TT, SHIFT, GH], bf16) for u in range(2)]
            rden = sb("rden", [P, TT, GH], fp32)
            stats = sb("stats", [P, TT, 6], fp32)
            meanvar = sb("meanvar", [P, TT, 2], fp32)
            vareps = sb("vareps", [P, TT], fp32)
            rstd = sb("rstd", [P, TT], fp32)
            mhalf = sb("mhalf", [P, TT], fp32)
            eps = sb("eps", [P, TT], fp32)
            wqk_hi = sb("wqk_hi", [P, DT, 2 * D], f32r)
            wqk_lo = sb("wqk_lo", [P, DT, 2 * D], f32r)
            wv_hi = sb("wv_hi", [P, DT, D + E], f32r)
            wv_lo = sb("wv_lo", [P, DT, D + E], f32r)
            wo_hi = sb("wo_hi", [P, DT, D], f32r)
            wo_lo = sb("wo_lo", [P, DT, D], f32r)
            vb_all = sb("vb_all", [P, D], fp32)
            ob_all = sb("ob_all", [P, D], fp32)
            rowmask = sb("rowmask", [P, T], fp32)
            colmask = sb("colmask", [P, P], bf16)
            fold_raw = [probs[w][:, 0:DT * H * R].rearrange("p (t h r) -> p t h r", t=DT, h=H) for w in range(2)]
            vw_raw = probs[0][:, 2048:2560].rearrange("p (t d) -> p t d", t=DT)
            ow_raw = probs[1][:, 2048:2560].rearrange("p (t d) -> p t d", t=DT)
            choice_raw = probs[0][0:E, 2560:2560 + D]
            foldb = probs[1][:, 2560:2560 + 2 * D].rearrange("p (w c j) -> p w c j", w=2, c=H // 2)
            fold_t = [probs[w][:, 3072:3584] for w in range(2)]

            dve_past, sp_past = sem("dve_past"), sem("sp_past")
            weights_in = sem("weights_in")
            consts = sem("consts")
            zeroed = sem("zeroed")
            foldb_zero = sem("foldb_zero")
            x_in = sem("x_in")
            stats_done = sem("stats_done")
            mv_done = sem("mv_done")
            vareps_done = sem("vareps_done")
            rstd_done = sem("rstd_done")
            xn_done = sem("xn_done")
            xn_stored = sem("xn_stored")
            shared_ready = [sem(f"shared_ready{u}") for u in range(2)]
            shared_done = [sem(f"shared_done{u}") for u in range(2)]
            hi_done = sem("hi_done")
            mid_done = sem("mid_done")
            lo_done = sem("lo_done")
            stacked = [sem(f"stacked{u}") for u in range(2)]
            logit_done = sem("logit_done")
            score_ready = sem("score_ready")
            score_done = sem("score_done")
            neghi_done = sem("neghi_done")
            negmax_done = sem("negmax_done")
            max_in = [sem(f"max_in{u}") for u in range(2)]
            scoret_ready = sem("scoret_ready")
            exp_done = sem("exp_done")
            pv_ready = sem("pv_ready")
            yraw_done = sem("yraw_done")
            rden_done = sem("rden_done")
            xres_in = sem("xres_in")
            xres_done = sem("xres_done")
            out_stored = sem("out_stored")

            SCORE, SCORET, Y, SHARED = banks[0:3], banks[3:5], banks[5], banks[6:8]
            FIRST, PER_PAIR = UN * 3, UN * GB * 2

            def score_bank(u):
                return (u if u < FIRST else (u - FIRST) % PER_PAIR) % 3

            def score_back(u):
                return next(d for d in range(1, 6) if score_bank(u - d) == score_bank(u))

            N_CONST = 10
            STACK_DMAS = 16 * 2 * len(TERMS)
            N_WEIGHTS = 16 * 13

            def program(eng, steps_fn):
                same = lambda value, per_pair: value
                steps_fn(prologue_steps() + pair_steps(0), same)
                with eng.Fori(1, PAIRS - 1) as i:
                    steps_fn(pair_steps(1), lambda value, per_pair: i * per_pair + (value - per_pair))
                steps_fn(pair_steps(PAIRS - 1) + epilogue_steps(), same)

            def bank_of(step):
                return unit_of[step] % 2

            def filled(step, at):
                return at(unit_of[step] // 2 + 1, U_PAIR // 2)

            def emptied(step, at):
                return at(unit_of[step] // 2 + 1, U_PAIR // 2)

            def split(step, at):
                return at(split_of[step] + 1, S_PAIR)

            block = mem.enter_context(nc.Block())

            @block.sync
            def _(sp):
                def steps(todo, at):
                    for step in todo:
                        kind, n, k = step
                        if kind == "xload":
                            if n >= 1:
                                sp.wait_ge(xn_done, at(n, 2))
                                sp.sem_inc(sp_past, 1)
                            sp.dma_start(xln[:], x_v[at(n, 2)]).then_inc(x_in, 16)
                        elif kind == "lnapply":
                            sp.wait_ge(xn_done, at(n + 1, 2))
                            sp.sem_inc(sp_past, 1)
                            sp.dma_start(xn_v[at(n, 2)], xn[:]).then_inc(xn_stored, 16)
                        elif kind == "mid" and k % 2 == 1:
                            if n >= 2 and k == 1:
                                sp.wait_ge(scoret_ready, at(UN * GB * (n - 1), 8 * UN))
                                sp.sem_inc(sp_past, 1)
                            sp.wait_ge(lo_done, at(GB * n + k + 1, 2 * GB))
                            side = k // 2
                            stk = (qstk, kstk)[side][n % 2]
                            for t, term in enumerate(TERMS):
                                sp.dma_start(stk[HD * t:HD * t + HD, :, :],
                                             qk_part[term[side]][:, 2 * side:2 * side + 2, :]).then_inc(stacked[n % 2], 16)
                        elif kind == "maxt":
                            sp.wait_ge(shared_done[bank_of(step)], emptied(step, at))
                            sp.sem_inc(sp_past, 1)
                            b, g = divmod(n, GB)
                            for s in range(SHIFT):
                                sp.dma_start(qstk[b % 2][KS + s:KS + s + 1, GH * g:GH * g + GH, :],
                                             maxrow[n % 2][GH * s:GH * s + GH, :]).then_inc(max_in[n % 2], 16)
                        elif kind == "xres":
                            if n >= 1:
                                sp.wait_ge(out_stored, at(16 * n, 32))
                                sp.sem_inc(sp_past, 1)
                            sp.dma_start(xres[:], x_v[at(n, 2)]).then_inc(xres_in, 16)
                        elif kind == "o" and k == TT - 1:
                            sp.wait_ge(shared_done[bank_of(step)], emptied(step, at))
                            sp.sem_inc(sp_past, 1)
                            sp.wait_ge(shared_done[bank_of(("o", n, TT - 2))], emptied(("o", n, TT - 2), at))
                            sp.sem_inc(sp_past, 1)
                            sp.dma_start(out_v[at(n, 2)], xres[:]).then_inc(out_stored, 16)

                program(sp, steps)
                sp.wait_ge(xn_stored, 16 * B)
                sp.wait_ge(out_stored, 16 * B)

            @block.gpsimd
            def _(pool):
                nc.gpsimd.memset(ident[:], 0.0).then_inc(zeroed, 1)
                nc.gpsimd.memset(ident_bf[:], 0.0).then_inc(zeroed, 1)
                nc.gpsimd.memset(colmask[:], 0.0).then_inc(zeroed, 1)
                nc.gpsimd.memset(rowmask[:], 0.0).then_inc(zeroed, 1)
                nc.gpsimd.memset(mhalf[:], -0.5).then_inc(consts, 1)
                nc.gpsimd.memset(eps[:], EPS).then_inc(consts, 1)
                pool.wait_ge(zeroed, 4)
                nc.gpsimd.affine_select(out=ident[:], in_=ident[:], compare_op=ALU.not_equal, fill=1.0, base=0,
                                        pattern=[[-1, P]], channel_multiplier=1).then_inc(consts, 1)
                nc.gpsimd.affine_select(out=ident_bf[:], in_=ident_bf[:], compare_op=ALU.not_equal, fill=1.0, base=0,
                                        pattern=[[-1, P]], channel_multiplier=1).then_inc(consts, 1)
                nc.gpsimd.affine_select(out=colmask[:], in_=colmask[:], compare_op=ALU.is_ge, fill=NEG, base=0,
                                        pattern=[[-1, P]], channel_multiplier=1).then_inc(consts, 1)
                nc.gpsimd.affine_select(out=rowmask[:, T - P:T], in_=rowmask[:, T - P:T], compare_op=ALU.is_ge,
                                        fill=NEG, base=0, pattern=[[-1, P]], channel_multiplier=1).then_inc(consts, 1)
                for u in range(2):
                    nc.gpsimd.memset(vaug[u][:, :, :, HD:2 * HD], 1.0).then_inc(consts, 1)
                pool.wait_ge(consts, N_CONST - 2)
                nc.gpsimd.memset(kstk[0][KS:KS + SHIFT, :, :], 1.0).then_inc(consts, 1)
                nc.gpsimd.memset(kstk[1][KS:KS + SHIFT, :, :], 1.0).then_inc(consts, 1)

                def steps(todo, at):
                    for step in todo:
                        kind, n, k = step
                        if kind == "lnstat" and k == 1:
                            pool.wait_ge(mv_done, at(n + 1, 2))
                            if n >= 1:
                                pool.wait_ge(xn_done, at(n, 2))
                            nc.gpsimd.tensor_tensor(vareps[:], meanvar[:, :, 1], eps[:], ALU.add).then_inc(vareps_done, 1)
                            pool.wait_ge(vareps_done, at(n + 1, 2))
                            nc.gpsimd.tensor_tensor(rstd[:], vareps[:], mhalf[:], ALU.pow).then_inc(rstd_done, 1)
                        elif kind == "mid":
                            pool.wait_ge(mid_done, at(GB * n + k + 1, 2 * GB))
                            if n >= 1:
                                pool.wait_ge(stacked[(n - 1) % 2], at(STACK_DMAS * ((n - 1) // 2 + 1), STACK_DMAS))
                            nc.gpsimd.tensor_tensor(qk_part[2][:, k, :], rest[k % 2][:], qk_part[1][:, k, :],
                                                    ALU.subtract).then_inc(lo_done, 1)
                        elif kind == "xres":
                            pool.wait_ge(xres_in, at(16 * (n + 1), 32))
                            if n == 0:
                                pool.wait_ge(weights_in, N_WEIGHTS)
                            nc.gpsimd.tensor_tensor(xres[:], xres[:], ob_all[:].unsqueeze(1).to_broadcast([P, TT, D]),
                                                    ALU.add).then_inc(xres_done, 1)

                program(pool, steps)

            @block.scalar
            def _(act):
                for w, raw in enumerate((q_a, k_a)):
                    for dt in range(DT):
                        act.dma_start(fold_raw[w][:, dt, :, :],
                                      raw[:, P * dt:P * dt + P, :].rearrange("h p r -> p h r")).then_inc(weights_in, 16)
                act.dma_start(vw_raw, v_w.rearrange("(t p) d -> p t d", p=P)).then_inc(weights_in, 16)
                act.dma_start(choice_raw, choice_w).then_inc(weights_in, 16)
                act.dma_start(vb_all[:], v_b.partition_broadcast(P)).then_inc(weights_in, 16)
                act.wait_ge(foldb_zero, 1)
                for w, raw in enumerate((q_b, k_b)):
                    for odd in range(2):
                        act.dma_start(foldb[R * odd:R * odd + R, w, :, HD * odd:HD * odd + HD],
                                      raw.rearrange("(c two) r j -> two r c j", two=2)[odd]).then_inc(weights_in, 16)
                act.dma_start(ow_raw, o_w.rearrange("(t p) d -> p t d", p=P)).then_inc(weights_in, 16)
                act.dma_start(ob_all[:], o_b.partition_broadcast(P)).then_inc(weights_in, 16)
                act.wait_ge(weights_in, N_WEIGHTS)

                def steps(todo, at):
                    for step in todo:
                        kind, n, k = step
                        if step in unit_of:
                            p, src = bank_of(step), SHARED[bank_of(step)]
                        if kind == "foldt":
                            act.wait_ge(shared_ready[p], filled(step, at))
                            nc.scalar.activation(fold_t[k], src[:], ACT.Copy).then_inc(shared_done[p], 1)
                        elif kind == "fold":
                            act.wait_ge(shared_ready[p], filled(step, at))
                            w, dt = divmod(n, DT)
                            nc.scalar.activation(
                                wqk_hi[:, dt, D * w:D * w + D].rearrange("p (m j h) -> p m h j", m=2, h=8),
                                src[:, 0:D].rearrange("p (h m j) -> p m h j", m=2, h=8), ACT.Copy).then_inc(hi_done, 1)
                        elif kind == "wv":
                            act.wait_ge(shared_ready[p], filled(step, at))
                            nc.scalar.activation(wv_hi[:, n, :], src[:, 0:D + E], ACT.Copy).then_inc(hi_done, 1)
                        elif kind == "wo":
                            act.wait_ge(shared_ready[p], filled(step, at))
                            nc.scalar.activation(wo_hi[:, n, :], src[:, 0:D], ACT.Copy).then_inc(hi_done, 1)
                        elif kind == "xt":
                            act.wait_ge(shared_ready[p], filled(step, at))
                            nc.scalar.activation(xt_hi[:, k, :], src[:], ACT.Copy).then_inc(hi_done, 1)
                        elif kind == "yt":
                            act.wait_ge(shared_ready[p], filled(step, at))
                            nc.scalar.activation(yt_hi[:, k, :], src[:], ACT.Copy).then_inc(hi_done, 1)
                        elif kind == "qk":
                            act.wait_ge(shared_ready[p], filled(step, at))
                            if n >= 1 and k == 0:
                                act.wait_ge(stacked[(n - 1) % 2], at(STACK_DMAS * ((n - 1) // 2 + 1), STACK_DMAS))
                            nc.scalar.activation(qk_part[0][:, k, :], src[:], ACT.Copy).then_inc(hi_done, 1)
                        elif kind == "mid":
                            qk = ("qk", n, k)
                            act.wait_ge(shared_done[bank_of(qk)], emptied(qk, at))
                            nc.scalar.activation(qk_part[1][:, k, :], rest[k % 2][:], ACT.Copy).then_inc(mid_done, 1)
                        elif kind == "v":
                            act.wait_ge(shared_ready[p], filled(step, at))
                            nc.scalar.activation(logits[:, k, at(n, 2), :], src[:, D:D + E], ACT.Copy).then_inc(logit_done, 1)
                        elif kind == "maxt":
                            act.wait_ge(shared_ready[p], filled(step, at))
                            if n >= 2:
                                act.wait_ge(max_in[n % 2], at(32 * (n // 2), 128))
                            nc.scalar.activation(maxrow[n % 2][:], src[:].bitcast(bf16)[0:2 * GH, 0:T], ACT.Copy)\
                                .then_inc(shared_done[p], 1)
                        elif kind == "scoret":
                            act.wait_ge(scoret_ready, at(UN * n + k + 1, 8 * UN))
                            if k == 0 and n >= 2:
                                act.wait_ge(pv_ready, at(n - 1, 8))
                            nc.scalar.activation(probs[n % 2][:, 512 * k:512 * k + 512], SCORET[k % 2][:], ACT.Exp,
                                                 scale=SCALE).then_inc(exp_done, 1)
                        elif kind == "pv" and k == TT - 1:
                            act.wait_ge(pv_ready, at(n + 1, 8))
                            nc.scalar.activation(yraw[n % 2][:], Y[:], ACT.Copy).then_inc(yraw_done, 1)

                program(act, steps)

            @block.vector
            def _(dve):
                nc.vector.memset(foldb, 0.0).then_inc(foldb_zero, 1)

                def take_low(step, at, low, whole, high):
                    p = bank_of(step)
                    dve.wait_ge(hi_done, split(step, at))
                    nc.vector.tensor_tensor(low, whole, high, ALU.subtract).then_inc(shared_done[p], 1)

                def steps(todo, at):
                    for step in todo:
                        kind, n, k = step
                        if step in unit_of:
                            p, src = bank_of(step), SHARED[bank_of(step)]
                        if kind == "lnstat":
                            dve.wait_ge(x_in, at(16 * (n + 1), 32))
                            for tt in (2 * k, 2 * k + 1):
                                last = nc.vector.bn_stats(stats[:, tt, :], xln[:, tt, :])
                            last.then_inc(stats_done, 1)
                            if k == 1:
                                dve.wait_ge(stats_done, at(2 * (n + 1), 4))
                                dve.sem_inc(dve_past, 1)
                                for tt in range(TT):
                                    last = nc.vector.bn_aggr(meanvar[:, tt, :], stats[:, tt, :])
                                last.then_inc(mv_done, 1)
                        elif kind == "lnapply":
                            dve.wait_ge(rstd_done, at(n + 1, 2))
                            if n >= 1:
                                dve.wait_ge(xn_stored, at(16 * n, 32))
                                prev = ("xt", n - 1, 1)
                                dve.wait_ge(shared_ready[bank_of(prev)], filled(prev, at))
                            for tt in range(TT):
                                last = nc.vector.tensor_scalar(xn[:, tt, :], xln[:, tt, :], meanvar[:, tt, 0:1],
                                                               rstd[:, tt:tt + 1], ALU.subtract, ALU.mult)
                            last.then_inc(xn_done, 1)
                        elif kind == "fold":
                            w, dt = divmod(n, DT)
                            view = "p (m j h) -> p m h j"
                            take_low(step, at, wqk_lo[:, dt, D * w:D * w + D].rearrange(view, m=2, h=8),
                                     src[:, 0:D].rearrange("p (h m j) -> p m h j", m=2, h=8),
                                     wqk_hi[:, dt, D * w:D * w + D].rearrange(view, m=2, h=8))
                        elif kind == "wv":
                            take_low(step, at, wv_lo[:, n, :], src[:, 0:D + E], wv_hi[:, n, :])
                        elif kind == "wo":
                            take_low(step, at, wo_lo[:, n, :], src[:, 0:D], wo_hi[:, n, :])
                        elif kind == "xt":
                            take_low(step, at, xt_lo[:, k, :], src[:], xt_hi[:, k, :])
                        elif kind == "yt":
                            take_low(step, at, yt_lo[:, k, :], src[:], yt_hi[:, k, :])
                        elif kind == "qk":
                            if 4 * n + k >= 2:
                                dve.wait_ge(lo_done, at(4 * n + k - 1, 8))
                            take_low(step, at, rest[k % 2][:], src[:], qk_part[0][:, k, :])
                        elif kind == "v":
                            dve.wait_ge(logit_done, at(4 * n + k + 1, 8))
                            nc.vector.tensor_tensor(vaug[n % 2][:, k, :, 0:HD],
                                                    src[:, 0:D].rearrange("p (h j) -> p h j", h=H),
                                                    vb_all[:].rearrange("p (h j) -> p h j", h=H), ALU.add)\
                                .then_inc(shared_done[p], 1)
                        elif kind == "score":
                            u = UN * n + k
                            dve.wait_ge(score_ready, at(u + 1, 8 * UN))
                            if u >= 2:
                                dve.wait_ge(score_done, at(u - 1, 8 * UN))
                            if k == 0 and n >= 2:
                                dve.wait_ge(negmax_done, at(n - 1, 8))
                            dve.sem_inc(dve_past, 1)
                            for h, i, col, width in unit_parts(k, False):
                                last = nc.vector.tensor_tensor_reduce(
                                    out=junk[k % 2][:, col:col + width], in0=SCORE[score_bank(UN * n + k)][:, col:col + width],
                                    in1=rowmask[:, T - width:T], scale=1.0, scalar=-3e38, op0=ALU.add, op1=ALU.max,
                                    accum_out=rowmax[n % 2][:, i, h:h + 1])
                            last.then_inc(score_done, 1)
                            if k == UN - 1:
                                if n >= 2:
                                    prev = ("maxt", n - 2, 0)
                                    dve.wait_ge(shared_ready[bank_of(prev)], filled(prev, at))
                                dve.wait_ge(score_done, at(u + 1, 8 * UN))
                                nc.vector.tensor_scalar(negmax[n % 2][:, :, 0, :], rowmax[n % 2][:], -1.0, None, ALU.mult)\
                                    .then_inc(neghi_done, 1)
                                dve.wait_ge(neghi_done, at(n + 1, 8))
                                nc.vector.scalar_tensor_tensor(out=negmax[n % 2][:, :, 1, :], in0=rowmax[n % 2][:],
                                                               scalar=-1.0, in1=negmax[n % 2][:, :, 0, :],
                                                               op0=ALU.mult, op1=ALU.subtract).then_inc(negmax_done, 1)
                        elif kind == "ytr":
                            dve.wait_ge(shared_ready[p], filled(step, at))
                            y4 = src[:].rearrange("p (q h c) -> p q h c", q=TT, h=GH)
                            if n >= 1:
                                prev = ("ytr", n - 1, 0)
                                dve.wait_ge(shared_done[bank_of(prev)], emptied(prev, at))
                            nc.vector.reciprocal(rden[:], y4[:, :, :, HD]).then_inc(rden_done, 1)
                            dve.wait_ge(rden_done, at(n + 1, 8))
                            if n % GB == 0 and n >= GB:
                                prev = ("yt", n // GB - 1, 1)
                                dve.wait_ge(shared_ready[bank_of(prev)], filled(prev, at))
                            g = n % GB
                            nc.vector.tensor_tensor(
                                ytok[:, :, GH * HD * g:GH * HD * (g + 1)].rearrange("p q (h c) -> p q h c", h=GH),
                                y4[:, :, :, 0:HD], rden[:].unsqueeze(3).to_broadcast([P, TT, GH, HD]), ALU.mult)\
                                .then_inc(shared_done[p], 1)
                        elif kind == "o":
                            dve.wait_ge(shared_ready[p], filled(step, at))
                            dve.wait_ge(xres_done, at(n + 1, 2))
                            nc.vector.tensor_tensor(xres[:, k, :], src[:, 0:D], xres[:, k, :], ALU.add).then_inc(shared_done[p], 1)

                dve.wait_ge(consts, N_CONST)
                program(dve, steps)

            @block.tensor
            def _(pe):
                pe.wait_ge(consts, N_CONST)
                pe.wait_ge(weights_in, N_WEIGHTS)

                def three_passes(dst, left_hi, left_lo, right_hi, right_lo):
                    todo = [(left(dt), right(dt)) for dt in range(DT)
                            for left, right in ((left_hi, right_hi), (left_hi, right_lo), (left_lo, right_hi))]
                    for m, (a, b) in enumerate(todo):
                        last = nc.tensor.matmul(dst, a, b, start=m == 0, stop=m == len(todo) - 1)
                    return last

                def qk_passes(dst, mt, dt):
                    cols = slice(P * mt, P * mt + P)
                    for m, (a, b) in enumerate(((wqk_hi, xt_hi), (wqk_hi, xt_lo), (wqk_lo, xt_hi))):
                        last = nc.tensor.matmul(dst, a[:, dt, cols], b[:, dt, :],
                                                start=dt == 0 and m == 0, stop=dt == DT - 1 and m == 2)
                    return last

                def await_units(step, sources, at):
                    other = [s for s in sources if bank_of(s) != bank_of(step)] if step in unit_of else sources
                    for u in range(2):
                        mine = [s for s in other if bank_of(s) == u]
                        if mine:
                            pe.wait_ge(shared_done[u], emptied(max(mine, key=unit_of.get), at))

                def steps(todo, at):
                    for step in todo:
                        kind, n, k = step
                        if kind == "qk_first":
                            step = ("qk", n, k)
                        if step in unit_of:
                            p, dst = bank_of(step), SHARED[bank_of(step)]
                            if unit_of[step] >= 2 and kind != "qk":
                                pe.wait_ge(shared_done[p], at(unit_of[step] // 2, U_PAIR // 2))
                        if kind == "foldt":
                            w, dt = divmod(n, DT)
                            for c in range(4):
                                h = 2 * (4 * k + c)
                                last = nc.tensor.transpose(dst[:, P * c:P * c + P],
                                                           fold_raw[w][:, dt, h:h + 2, :].rearrange("p h r -> p (h r)"), ident[:])
                            last.then_inc(shared_ready[p], 1)
                        elif kind == "fold":
                            await_units(step, [("foldt", n, half) for half in range(2)], at)
                            for c in range(H // 2):
                                last = nc.tensor.matmul(dst[:, 2 * HD * c:2 * HD * c + 2 * HD],
                                                        fold_t[c // 4][:, P * (c % 4):P * (c % 4) + P],
                                                        foldb[:, n // DT, c, :], start=True, stop=True)
                            last.then_inc(shared_ready[p], 1)
                        elif kind == "wv":
                            for t in range(DT):
                                nc.tensor.transpose(dst[:, P * t:P * t + P], vw_raw[:, t, P * n:P * n + P], ident[:])
                            nc.tensor.transpose(dst[:, D:D + E], choice_raw[:, P * n:P * n + P], ident[0:E, 0:E])\
                                .then_inc(shared_ready[p], 1)
                        elif kind == "wo":
                            for t in range(DT):
                                last = nc.tensor.transpose(dst[:, P * t:P * t + P], ow_raw[:, t, P * n:P * n + P], ident[:])
                            last.then_inc(shared_ready[p], 1)
                        elif kind == "xt":
                            pe.wait_ge(xn_done, at(n + 1, 2))
                            for tt in range(TT):
                                last = nc.tensor.transpose(dst[:, P * tt:P * tt + P], xn[:, tt, P * k:P * k + P], ident[:])
                            last.then_inc(shared_ready[p], 1)
                        elif kind == "qk_first":
                            await_units(step, [("xt", n, dt) for dt in range(DT)]
                                        + [("fold", w, 0) for w in range(2 * DT) if n == 0], at)
                            qk_passes(dst[:], k, 0)
                        elif kind == "qk":
                            qk_passes(dst[:], k, 1).then_inc(shared_ready[p], 1)
                        elif kind == "v":
                            await_units(step, [("wv", dt, 0) for dt in range(DT) if n == 0], at)
                            rows = slice(P * k, P * k + P)
                            three_passes(dst[:, 0:D + E], lambda dt: xt_hi[:, dt, rows], lambda dt: xt_lo[:, dt, rows],
                                         lambda dt: wv_hi[:, dt, :], lambda dt: wv_lo[:, dt, :]).then_inc(shared_ready[p], 1)
                        elif kind == "score":
                            u, (b, g) = UN * n + k, divmod(n, GB)
                            if u >= 3:
                                pe.wait_ge(score_done, at(u - score_back(u) + 1, 8 * UN))
                            if g == 0 and k == 0:
                                pe.wait_ge(stacked[b % 2], at(STACK_DMAS * (b // 2 + 1), STACK_DMAS))
                            for h, i, col, width in unit_parts(k, False):
                                last = nc.tensor.matmul(SCORE[score_bank(UN * n + k)][:, col:col + width],
                                                        qstk[b % 2][0:KS, GH * g + h, P * i:P * i + P],
                                                        kstk[b % 2][0:KS, GH * g + h, 0:width], start=True, stop=True)
                            last.then_inc(score_ready, 1)
                        elif kind == "maxt":
                            pe.wait_ge(negmax_done, at(n + 1, 8))
                            for i in range(TT):
                                last = nc.tensor.transpose(dst[:].bitcast(bf16)[0:2 * GH, P * i:P * i + P],
                                                           negmax[n % 2][:, i, :, :].rearrange("p s h -> p (s h)"), ident_bf[:])
                            last.then_inc(shared_ready[p], 1)
                        elif kind == "scoret":
                            u, (b, g) = UN * n + k, divmod(n, GB)
                            if u >= 2:
                                pe.wait_ge(exp_done, at(u - 1, 8 * UN))
                            if k == 0:
                                pe.wait_ge(max_in[n % 2], at(32 * (n // 2 + 1), 128))
                            for h, j, col, width in unit_parts(k, True):
                                nc.tensor.matmul(SCORET[k % 2][:, col:col + width],
                                                 kstk[b % 2][0:KS + SHIFT, GH * g + h, P * j:P * j + P],
                                                 qstk[b % 2][0:KS + SHIFT, GH * g + h, P * j:T], start=True, stop=False)
                                last = nc.tensor.matmul(SCORET[k % 2][:, col:col + P], colmask[:], ident_bf[:],
                                                        start=False, stop=True)
                            last.then_inc(scoret_ready, 1)
                        elif kind == "pv":
                            b, g = divmod(n, GB)
                            if k == 0:
                                pe.wait_ge(exp_done, at(UN * (n + 1), 8 * UN))
                                if g == 0:
                                    await_units(step, [("v", b, tt) for tt in range(TT)], at)
                                if n >= 1:
                                    pe.wait_ge(yraw_done, at(n, 8))
                            where = {(h, j): (512 * t + col, width) for t in range(UN)
                                     for h, j, col, width in unit_parts(t, True)}
                            for h in range(GH):
                                col, width = where[h, k]
                                last = nc.tensor.matmul(Y[2 * HD * h:2 * HD * h + 2 * HD, P * k:T],
                                                        vaug[b % 2][:, k, GH * g + h, :],
                                                        probs[n % 2][:, col:col + width],
                                                        start=k == 0, stop=k == TT - 1)
                            if k == TT - 1:
                                last.then_inc(pv_ready, 1)
                        elif kind == "ytr":
                            pe.wait_ge(yraw_done, at(n + 1, 8))
                            for i in range(TT):
                                last = nc.tensor.transpose(dst[:, P * i:P * i + P], yraw[n % 2][:, P * i:P * i + P], ident[:])
                            last.then_inc(shared_ready[p], 1)
                        elif kind == "yt":
                            await_units(step, [("ytr", GB * n + g, 0) for g in range(GB)], at)
                            for tt in range(TT):
                                last = nc.tensor.transpose(dst[:, P * tt:P * tt + P], ytok[:, tt, P * k:P * k + P], ident[:])
                            last.then_inc(shared_ready[p], 1)
                        elif kind == "o":
                            await_units(step, [("yt", n, dt) for dt in range(DT)]
                                        + [("wo", dt, 0) for dt in range(DT) if n == 0], at)
                            rows = slice(P * k, P * k + P)
                            three_passes(dst[:, 0:D], lambda dt: yt_hi[:, dt, rows], lambda dt: yt_lo[:, dt, rows],
                                         lambda dt: wo_hi[:, dt, :], lambda dt: wo_lo[:, dt, :]).then_inc(shared_ready[p], 1)

                program(pe, steps)

        experts(nc, sem, ident, logits, banks, xn_dram, out_rows, w1, w2)


def expert_steps(e):
    out = []
    for grp in range(EG):
        n = EG * e + grp
        out += [("h", n, ft) for ft in range(FT)]
        if grp == EG - 1 and e + 1 < E:
            out.append(("w1", e + 1, 0))
        if n + 1 < E * EG:
            out += [("pick", n + 1, dt) for dt in range(DT)]
        if n + 3 < E * EG:
            out.append(("gather", n + 3, 0))
        out += [("down", n, j) for j in range(GB4 // 2)]
        if grp == EG - 1 and e + 1 < E:
            out.append(("w2", e + 1, 0))
    return out


def experts(nc, sem, ident, logits, banks, xn_dram, out_rows, w1, w2):
    fp32, f32r = mybir.dt.float32, mybir.dt.float32r
    i32, u32 = mybir.dt.int32, mybir.dt.uint32
    ALU, ACT, AX = mybir.AluOpType, mybir.ActivationFunctionType, mybir.AxisListType
    BE = B * E
    assert BE == P and CAP == P
    w1_v = w1.rearrange("e (t p) f -> e p t f", p=P)
    w2_v = w2.rearrange("e (t p) d -> e p t d", p=P)
    start_steps = [("w1", 0, 0), ("w2", 0, 0), ("gather", 0, 0), ("gather", 1, 0),
                   ("pick", 0, 0), ("pick", 0, 1), ("gather", 2, 0)]

    with ExitStack() as mem:
        def sb(name, shape, dt):
            return mem.enter_context(nc.sbuf_tensor(name, shape, dt))

        gate = sb("gate", [P, TT, BE], fp32)
        gsum = sb("gsum", [P, TT * B], fp32)
        ranked = [sb(f"ranked{u}", [P, T], fp32) for u in range(2)]
        top = sb("top", [P, CAP], fp32)
        top_at = sb("top_at", [P, CAP], u32)
        top_row = sb("top_row", [P, CAP], fp32)
        first_i = [sb(f"first_i{u}", [P, 1], i32) for u in range(3)]
        first = sb("first", [P, 1], fp32)
        rows = sb("rows", [P, B, E], u32)
        gates = sb("gates", [P, B, E], fp32)
        row_sel = [sb(f"row_sel{g}", [P, GB4, 1], u32) for g in range(EG)]
        gate_sel = [sb(f"gate_sel{g}", [P, GB4, 1], fp32) for g in range(EG)]
        w1_raw = sb("w1_raw", [P, DT, F], fp32)
        w2_raw = sb("w2_raw", [P, FT, D], fp32)
        w1_hi, w1_lo = sb("w1_hi", [P, DT, F], f32r), sb("w1_lo", [P, DT, F], f32r)
        w2_hi, w2_lo = sb("w2_hi", [P, FT, D], f32r), sb("w2_lo", [P, FT, D], f32r)
        picked = [sb(f"picked{u}", [P, GB4, D], fp32) for u in range(2)]
        pt_hi, pt_lo = sb("pt_hi", [P, DT, T], f32r), sb("pt_lo", [P, DT, T], f32r)
        hid = [sb(f"hid{u}", [P, T], fp32) for u in range(2)]
        hid_hi, hid_lo = sb("hid_hi", [P, FT, T], f32r), sb("hid_lo", [P, FT, T], f32r)
        mixed = [sb(f"mixed{u}", [P, GB4, D], fp32) for u in range(2)]
        PICK, UP, DOWN = banks[0:2], banks[2:6], banks[6:8]

        pool_past, sp_past = sem("pool_past2"), sem("sp_past2")
        gate_step = sem("gate_step")
        gate_exp = sem("gate_exp")
        ids = sem("ids")
        rank_ready = sem("rank_ready")
        rank_done = sem("rank_done")
        w1_in, w2_in = sem("w1_in"), sem("w2_in")
        w1_high, w2_high = sem("w1_high"), sem("w2_high")
        w1_done, w2_done = sem("w1_done"), sem("w2_done")
        sel_done = sem("sel_done")
        gathered = [sem(f"gathered{g}") for g in range(EG)]
        pick_ready, pick_hi, pick_done = sem("pick_ready"), sem("pick_hi"), sem("pick_done")
        up_ready, silu_done, hid_high, hid_done = sem("up_ready"), sem("silu_done"), sem("hid_high"), sem("hid_done")
        down_ready, mixed_done = sem("down_ready"), sem("mixed_done")
        added = [sem(f"added{g}") for g in range(EG)]

        def program(eng, steps_fn):
            same = lambda value, per_expert: value
            steps_fn(start_steps + expert_steps(0), same)
            with eng.Fori(1, E - 1) as e:
                steps_fn(expert_steps(1), lambda value, per_expert: e * per_expert + (value - per_expert))
            steps_fn(expert_steps(E - 1), same)

        block = mem.enter_context(nc.Block())

        @block.sync
        def _(sp):
            def steps(todo, at):
                for kind, n, k in todo:
                    if kind == "w1":
                        if n >= 1:
                            sp.wait_ge(w1_done, at(n, 1))
                            sp.sem_inc(sp_past, 1)
                        sp.dma_start(w1_raw[:], w1_v[at(n, 1)]).then_inc(w1_in, 16)
                    elif kind == "w2":
                        if n >= 1:
                            sp.wait_ge(w2_done, at(n, 1))
                            sp.sem_inc(sp_past, 1)
                        sp.dma_start(w2_raw[:], w2_v[at(n, 1)]).then_inc(w2_in, 16)

            def ahead(todo, at):
                steps([(kind, n, k) for kind, n, k in todo if kind in ("w1", "w2")], at)

            program(sp, ahead)

        @block.gpsimd
        def _(pool):
            nc.gpsimd.iota(first_i[0][:], pattern=[[0, 1]], base=0, channel_multiplier=1).then_inc(ids, 1)

            def steps(todo, at):
                for kind, n, k in todo:
                    grp = n % EG
                    if kind == "gather":
                        pool.wait_ge(sel_done, at(n + 1, EG))
                        if n >= 2:
                            pool.wait_ge(pick_ready, at(DT * (n - 1), EG * DT))
                        pool.sem_inc(pool_past, 1)
                        for j in range(GB4):
                            nc.gpsimd.indirect_dma_start(
                                out=picked[n % 2][:, j, :], out_offset=None, in_=xn_dram,
                                in_offset=bass.IndirectOffsetOnAxis(ap=row_sel[grp][:, j, :], axis=0)).then_inc(gathered[grp], 16)
                    elif kind == "down" and k == GB4 // 2 - 1:
                        pool.wait_ge(mixed_done, at((GB4 // 2) * (n + 1), EG * GB4 // 2))
                        if n >= EG:
                            pool.wait_ge(added[grp], at(16 * GB4 * (n // EG), 16 * GB4))
                        pool.sem_inc(pool_past, 1)
                        for j in range(GB4):
                            nc.gpsimd.indirect_dma_start(
                                out=out_rows, out_offset=bass.IndirectOffsetOnAxis(ap=row_sel[grp][:, j, :], axis=0),
                                in_=mixed[n % 2][:, j, :], in_offset=None, compute_op=ALU.add).then_inc(added[grp], 16)

            program(pool, steps)
            for g in range(EG):
                pool.wait_ge(added[g], 16 * GB4 * E)

        @block.scalar
        def _(act):
            act.wait_ge(gate_step, 2)
            nc.scalar.activation(gate[:], gate[:], ACT.Exp).then_inc(gate_exp, 1)
            act.wait_ge(rank_ready, 1)
            nc.scalar.activation(ranked[0][:], PICK[0][:], ACT.Copy).then_inc(rank_done, 1)

            def steps(todo, at):
                for kind, n, k in todo:
                    if kind == "w1":
                        act.wait_ge(w1_in, at(16 * (n + 1), 16))
                        if n >= 1:
                            act.wait_ge(up_ready, at(FT * EG * n, FT * EG))
                        nc.scalar.activation(w1_hi[:], w1_raw[:], ACT.Copy).then_inc(w1_high, 1)
                    elif kind == "w2":
                        act.wait_ge(w2_in, at(16 * (n + 1), 16))
                        if n >= 1:
                            act.wait_ge(down_ready, at(GB4 // 2 * EG * n, GB4 // 2 * EG))
                        nc.scalar.activation(w2_hi[:], w2_raw[:], ACT.Copy).then_inc(w2_high, 1)
                    elif kind == "pick":
                        act.wait_ge(pick_ready, at(DT * n + k + 1, DT * EG))
                        nc.scalar.activation(pt_hi[:, k, :], PICK[k][:], ACT.Copy).then_inc(pick_hi, 1)
                    elif kind == "h":
                        act.wait_ge(up_ready, at(FT * n + k + 1, FT * EG))
                        if FT * n + k >= 2:
                            act.wait_ge(hid_done, at(FT * n + k - 1, FT * EG))
                        nc.scalar.activation(hid[k % 2][:], UP[k][:], ACT.Silu).then_inc(silu_done, 1)

            program(act, steps)

        @block.vector
        def _(dve):
            count = [0]

            def then(ins):
                count[0] += 1
                ins.then_inc(gate_step, 1)
                dve.wait_ge(gate_step, count[0])

            by_e = lambda t: t[:].rearrange("p t (b e) -> p (t b) e", e=E)
            log_v = logits[:].rearrange("p t b e -> p (t b) e")
            over_e = gsum[:].unsqueeze(2).to_broadcast([P, TT * B, E])
            then(nc.vector.reduce_max(gsum[:], log_v, AX.X))
            then(nc.vector.tensor_tensor(by_e(gate), log_v, over_e, ALU.subtract))
            dve.wait_ge(gate_exp, 1)
            then(nc.vector.reduce_sum(gsum[:], by_e(gate), AX.X))
            then(nc.vector.reciprocal(gsum[:], gsum[:]))
            then(nc.vector.tensor_tensor(by_e(gate), by_e(gate), over_e, ALU.mult))
            dve.wait_ge(ids, 1)
            then(nc.vector.tensor_single_scalar(first_i[1][:], first_i[0][:], 3, ALU.arith_shift_right))
            then(nc.vector.tensor_single_scalar(first_i[2][:], first_i[1][:], 9, ALU.logical_shift_left))
            then(nc.vector.tensor_copy(first[:], first_i[2][:]))
            dve.wait_ge(rank_done, 1)
            for r in range(CAP // 8):
                src, dst, eight = ranked[r % 2], ranked[(r + 1) % 2], slice(8 * r, 8 * r + 8)
                then(nc.vector.max(top[:, eight], src[:]))
                then(nc.vector.max_index(top_at[:, eight], top[:, eight], src[:]))
                if r + 1 < CAP // 8:
                    then(nc.vector.match_replace(dst[:], top[:, eight], src[:], -1.0))
            then(nc.vector.tensor_copy(top_row[:], top_at[:]))
            then(nc.vector.tensor_scalar(top_row[:], top_row[:], first[:], None, ALU.add))
            dve.wait_ge(rank_ready, 2)
            be = lambda t: t[:].rearrange("p b e -> p (b e)")
            then(nc.vector.tensor_copy(be(rows), PICK[1][:, 0:P]))
            then(nc.vector.tensor_copy(be(gates), PICK[1][:, P:2 * P]))

            def steps(todo, at):
                for kind, n, k in todo:
                    grp = n % EG
                    if kind == "w1":
                        dve.wait_ge(w1_high, at(n + 1, 1))
                        nc.vector.tensor_tensor(w1_lo[:], w1_raw[:], w1_hi[:], ALU.subtract).then_inc(w1_done, 1)
                    elif kind == "w2":
                        dve.wait_ge(w2_high, at(n + 1, 1))
                        nc.vector.tensor_tensor(w2_lo[:], w2_raw[:], w2_hi[:], ALU.subtract).then_inc(w2_done, 1)
                    elif kind == "gather":
                        if n >= EG:
                            dve.wait_ge(added[grp], at(16 * GB4 * (n // EG), 16 * GB4))
                        of = slice(GB4 * grp, GB4 * grp + GB4)
                        e = at(n // EG, 1)
                        nc.vector.tensor_copy(gate_sel[grp][:], gates[:, of, bass.ds(e, 1)])
                        nc.vector.tensor_copy(row_sel[grp][:], rows[:, of, bass.ds(e, 1)]).then_inc(sel_done, 1)
                    elif kind == "pick":
                        dve.wait_ge(pick_hi, at(DT * n + k + 1, DT * EG))
                        nc.vector.tensor_tensor(pt_lo[:, k, :], PICK[k][:], pt_hi[:, k, :], ALU.subtract).then_inc(pick_done, 1)
                    elif kind == "h":
                        u = FT * n + k
                        dve.wait_ge(silu_done, at(u + 1, FT * EG))
                        nc.vector.tensor_copy(hid_hi[:, k, :], hid[k % 2][:]).then_inc(hid_high, 1)
                        dve.wait_ge(hid_high, at(u + 1, FT * EG))
                        nc.vector.tensor_tensor(hid_lo[:, k, :], hid[k % 2][:], hid_hi[:, k, :], ALU.subtract).then_inc(hid_done, 1)
                    elif kind == "down":
                        u = GB4 // 2 * n + k
                        dve.wait_ge(down_ready, at(u + 1, GB4 // 2 * EG))
                        dve.wait_ge(sel_done, at(n + 1, EG))
                        if n >= 2 and k == 0:
                            dve.wait_ge(added[(n - 2) % EG], at(16 * GB4 * ((n - 2) // EG + 1), 16 * GB4))
                        for t in range(2):
                            j = 2 * k + t
                            last = nc.vector.tensor_scalar(mixed[n % 2][:, j, :], DOWN[k][:, D * t:D * t + D],
                                                           gate_sel[grp][:, j, :], None, ALU.mult)
                        last.then_inc(mixed_done, 1)

            program(dve, steps)

        @block.tensor
        def _(pe):
            pe.wait_ge(gate_step, 5)
            for tt in range(TT):
                last = nc.tensor.transpose(PICK[0][:, P * tt:P * tt + P], gate[:, tt, :], ident[:])
            last.then_inc(rank_ready, 1)
            pe.wait_ge(gate_step, 8 + 3 * (CAP // 8) - 1 + 2)
            nc.tensor.transpose(PICK[1][:, 0:P], top_row[:], ident[:])
            nc.tensor.transpose(PICK[1][:, P:2 * P], top[:], ident[:]).then_inc(rank_ready, 1)
            pe.wait_ge(gate_step, 8 + 3 * (CAP // 8) - 1 + 4)

            def steps(todo, at):
                for kind, n, k in todo:
                    if kind == "pick":
                        if k == 0:
                            pe.wait_ge(gathered[n % EG], at(16 * GB4 * (n // EG + 1), 16 * GB4))
                        if n >= 1:
                            pe.wait_ge(pick_done, at(DT * (n - 1) + k + 1, DT * EG))
                        for j in range(GB4):
                            last = nc.tensor.transpose(PICK[k][:, P * j:P * j + P], picked[n % 2][:, j, P * k:P * k + P], ident[:])
                        last.then_inc(pick_ready, 1)
                    elif kind == "h":
                        u = FT * n + k
                        if k == 0:
                            pe.wait_ge(pick_done, at(DT * (n + 1), DT * EG))
                            if n % EG == 0:
                                pe.wait_ge(w1_done, at(n // EG + 1, 1))
                        if n >= 1:
                            pe.wait_ge(silu_done, at(u - FT + 1, FT * EG))
                        f = slice(P * k, P * k + P)
                        todo_mm = [(a[:, dt, f], b[:, dt, :]) for dt in range(DT)
                                   for a, b in ((w1_hi, pt_hi), (w1_hi, pt_lo), (w1_lo, pt_hi))]
                        for m, (a, b) in enumerate(todo_mm):
                            last = nc.tensor.matmul(UP[k][:], a, b, start=m == 0, stop=m == len(todo_mm) - 1)
                        last.then_inc(up_ready, 1)
                    elif kind == "down":
                        u = GB4 // 2 * n + k
                        if k == 0:
                            pe.wait_ge(hid_done, at(FT * (n + 1), FT * EG))
                            if n % EG == 0:
                                pe.wait_ge(w2_done, at(n // EG + 1, 1))
                        if n >= 1:
                            pe.wait_ge(mixed_done, at(u - 1, GB4 // 2 * EG))
                        for t in range(2):
                            r = slice(P * (2 * k + t), P * (2 * k + t) + P)
                            todo_mm = [(a[:, ft, r], b[:, ft, :]) for ft in range(FT)
                                       for a, b in ((hid_hi, w2_hi), (hid_hi, w2_lo), (hid_lo, w2_hi))]
                            for m, (a, b) in enumerate(todo_mm):
                                last = nc.tensor.matmul(DOWN[k][:, D * t:D * t + D], a, b, start=m == 0, stop=m == len(todo_mm) - 1)
                        last.then_inc(down_ready, 1)

            program(pe, steps)


_INS = ["L0_attn_hidden_states", "L0_attn_q_a", "L0_attn_q_b", "L0_attn_k_a", "L0_attn_k_b", "L0_attn_v_w",
        "L0_attn_v_b", "L0_attn_o_w", "L0_attn_o_b", "L0_ffn_choice_w", "L0_ffn_w1", "L0_ffn_w2"]


def kernel(**inputs):
    import numpy as np
    import concourse.bacc as bacc
    from concourse.bass_utils import run_bass_kernel_spmd

    nc = bacc.Bacc("TRN2", target_bir_lowering=False, num_devices=1)
    arrays, args = {}, []
    for name in _INS:
        a = np.ascontiguousarray(inputs[name])
        arrays[f"in_{name}"] = a
        args.append(nc.dram_tensor(f"in_{name}", a.shape, mybir.dt.from_np(a.dtype), kind="ExternalInput").ap())
    out = nc.dram_tensor("out_rows", (B, T, D), mybir.dt.float32, kind="ExternalOutput").ap()
    build(nc, *args, out)
    r = run_bass_kernel_spmd(nc, [arrays], core_ids=[0])
    return r.results[0]["out_rows"]
```

```python
import concourse.bass as bass
from concourse import mybir
from contextlib import ExitStack

B, T, D = 16, 512, 256
H, HD, R = 16, 16, 64
E, F = 8, 512
CAP = T * 2 // E
P = 128
TT, DT, FT = T // P, D // P, F // P
EPS = 1e-5
GH = 4
GB = H // GH
NG = B * GB
UN = 10
TERMS = ((0, 0), (0, 1), (1, 0), (0, 2), (2, 0), (1, 1))
KS = HD * len(TERMS)
SHIFT = 2
NEG = -1e30
GB4 = 4
EG = B // GB4
SCALE = 1.0 / HD ** 0.5


def unit_parts(t, transposed):
    pair, r = divmod(t, 5)
    a, b = 2 * pair, 2 * pair + 1
    parts = [[(a, 3)], [(a, 2), (a, 0)], [(a, 1), (b, 1)], [(b, 3)], [(b, 2), (b, 0)]][r]
    out, col = [], 0
    for h, i in parts:
        out.append((h, 3 - i if transposed else i, col, P * (i + 1)))
        col += P * (i + 1)
    return out


def slot_steps(b, g):
    G = GB * b + g
    put = {t: [] for t in range(UN)}
    for t, j in zip((2, 3, 4, 5), range(TT)):
        put[t].append(("pv", G, j))
    if G + 2 < NG:
        put[4].append(("maxt", G + 2, 0))
    if g == 0:
        if b + 2 < B:
            put[0].append(("xload", b + 2, 0))
            put[9].append(("lnstat", b + 2, 0))
        if b >= 1 and b + 1 < B:
            put[1].append(("mid", b + 1, 3))
        if b + 1 < B:
            for t, tt in zip((0, 8, 9), range(TT)):
                put[t].append(("v", b + 1, tt))
        if b >= 1:
            put[1].append(("yt", b - 1, 0))
            put[6].append(("yt", b - 1, 1))
    elif g == 1:
        if b + 1 < B:
            put[0].append(("v", b + 1, 3))
        if b >= 1:
            for t, tt in zip((1, 6, 8, 9), range(TT)):
                put[t].append(("o", b - 1, tt))
        if b + 2 < B:
            put[2].append(("lnstat", b + 2, 1))
            put[8].append(("lnapply", b + 2, 0))
    elif g == 2:
        put[1].append(("xres", b, 0))
        if b + 2 < B:
            put[0].append(("xt", b + 2, 0))
            put[1].append(("xt", b + 2, 1))
            put[6].append(("qk_first", b + 2, 0))
            put[8].append(("qk", b + 2, 0))
            put[9].append(("qk_first", b + 2, 1))
    elif g == 3 and b + 2 < B:
        put[0] += [("qk", b + 2, 1), ("mid", b + 2, 0)]
        put[1].append(("qk_first", b + 2, 2))
        put[2].append(("mid", b + 2, 1))
        put[6].append(("qk", b + 2, 2))
        put[8] += [("qk_first", b + 2, 3), ("mid", b + 2, 2)]
        put[9].append(("qk", b + 2, 3))
    put[7].append(("ytr", G, 0))
    for t, step in routing_steps(G):
        put[t].append(step)
    out = []
    for t in range(UN):
        out += [("scoret", G + 1, t)] * (G + 1 < NG) + [("score", G + 3, t)] * (G + 3 < NG) + put[t]
    return out


RANK_OPS = 3 * (CAP // 8) - 1


def routing_steps(G):
    left = NG - G
    if left == 7:
        return [(3, ("gate_max", 0, 0)), (4, ("gate_exp", 0, 0)), (6, ("gate_norm", 0, 0)), (8, ("rankt", 0, 0))]
    out, per_slot = [], {6: (0, 1, 3, 4, 6, 7, 9), 5: (0, 1, 3, 4, 6, 7, 9), 4: (0, 1, 3, 4, 6, 7, 9),
                         3: range(9), 2: range(9), 1: range(8)}
    done = sum(len(places) for later, places in per_slot.items() if later > left)
    if left in per_slot:
        out += [(t, ("rank", done + m, 0)) for m, t in enumerate(per_slot[left])]
        assert left > 1 or done + len(per_slot[1]) == RANK_OPS
    if left == 5:
        out += [(0, ("w_load", 0, 0))]
    if left == 1:
        out += [(9, ("rows", 0, 0))]
    return out


def prologue_steps():
    out = [("xload", 0, 0), ("lnstat", 0, 0), ("lnstat", 0, 1), ("lnapply", 0, 0), ("xload", 1, 0)]
    transposed = [[("foldt", n, half) for half in range(2)] for n in range(2 * DT)]
    out += transposed[0] + transposed[1]
    for n in range(2 * DT):
        out += [("fold", n, 0)] + (transposed[n + 2] if n + 2 < 2 * DT else [])
    out += [("lnstat", 1, 0), ("lnstat", 1, 1)] + [("xt", 0, dt) for dt in range(DT)] + [("lnapply", 1, 0)]
    out += [("wv", dt, 0) for dt in range(DT)]
    for mt in (0, 2):
        out += [("qk_first", 0, mt), ("qk", 0, mt), ("qk_first", 0, mt + 1), ("qk", 0, mt + 1)]
        out += [("mid", 0, mt), ("v", 0, mt), ("mid", 0, mt + 1), ("v", 0, mt + 1)]
    out += [("xt", 1, dt) for dt in range(DT)] + [("wo", dt, 0) for dt in range(DT)]
    for mt in range(2):
        out += [("qk_first", 1, mt), ("qk", 1, mt), ("mid", 1, mt)]
    for t in range(UN):
        out.append(("score", 0, t))
        if t in (1, 4):
            out += [("qk_first", 1, 2 + t // 3), ("qk", 1, 2 + t // 3)]
        if t in (3, 6):
            out.append(("mid", 1, 1 + t // 3))
    for t in range(UN):
        out += [("score", 1, t)] + [("maxt", 0, 0)] * (t == 3)
    for t in range(UN):
        out += [("scoret", 0, t), ("score", 2, t)] + [("maxt", 1, 0)] * (t == 3)
    return out


def epilogue_steps():
    return [("yt", B - 1, 0), ("rowst", 0, 0), ("gather", 0, 0), ("yt", B - 1, 1)] \
        + [("o", B - 1, tt) for tt in range(TT)]


def pair_steps(i):
    return [s for b in (2 * i, 2 * i + 1) for g in range(GB) for s in slot_steps(b, g)]


class Handover:

    def __init__(self, rows, gates, row_sel, gate_sel, w_raw, picked, w_in, w_view, sel_done, gathered, out_stored):
        self.rows = rows
        self.gates = gates
        self.row_sel = row_sel
        self.gate_sel = gate_sel
        self.w_raw = w_raw
        self.picked = picked
        self.w_in = w_in
        self.w_view = w_view
        self.sel_done = sel_done
        self.gathered = gathered
        self.out_stored = out_stored


def build(nc, x, q_a, q_b, k_a, k_b, v_w, v_b, o_w, o_b, choice_w, w1, w2, out):
    fp32, f32r, bf16 = mybir.dt.float32, mybir.dt.float32r, mybir.dt.bfloat16
    i32, u32 = mybir.dt.int32, mybir.dt.uint32
    ALU, ACT, AX = mybir.AluOpType, mybir.ActivationFunctionType, mybir.AxisListType

    PAIRS = B // 2
    every = prologue_steps() + [s for i in range(PAIRS) for s in pair_steps(i)] + epilogue_steps()
    shared = [s for s in every if s[0] in ("foldt", "fold", "wv", "wo", "xt", "qk", "v", "maxt", "ytr", "yt", "o",
                                            "rankt", "rowst")]
    unit_of = {s: n for n, s in enumerate(shared)}
    split_of = {s: n for n, s in enumerate(s for s in shared if s[0] in ("fold", "wv", "wo", "xt", "qk", "yt"))}
    U_PAIR, S_PAIR = 48, 16
    for i in range(1, PAIRS - 2):
        for s, z in zip(pair_steps(i), pair_steps(i + 1)):
            assert s not in unit_of or unit_of[z] - unit_of[s] == U_PAIR
            assert s not in split_of or split_of[z] - split_of[s] == S_PAIR

    x_v = x.rearrange("b (t p) d -> b p t d", p=P)
    out_v = out.rearrange("b (t p) d -> b p t d", p=P)
    out_rows = out.rearrange("b t d -> (b t) d")
    xn_dram = nc.dram_tensor("xn_rows", (B * T, D), fp32, kind="Internal").ap()
    xn_v = xn_dram.rearrange("(b t p) d -> b p t d", b=B, p=P)

    ctx = ExitStack()
    with ctx:
        def sem(name):
            return ctx.enter_context(nc.semaphore(name))

        def keep(name, shape, dt):
            return ctx.enter_context(nc.sbuf_tensor(name, shape, dt))

        ident = keep("ident", [P, P], fp32)
        ident_bf = keep("ident_bf", [P, P], bf16)
        logits = keep("logits", [P, TT, B, E], fp32)
        qstk, kstk = [keep("qstk0", [P, H, T], bf16)], [keep("kstk0", [P, H, T], bf16)]
        xres = keep("xres", [P, TT, D], fp32)
        stack32 = [t[0][:].rearrange("p h t -> p (h t)").bitcast(fp32) for t in (qstk, kstk)]
        quarter = lambda which, n: stack32[which][:, 1024 * n:1024 * n + 1024]
        rows = keep("rows", [P, B, E], u32)
        gates = keep("gates", [P, B, E], fp32)
        moe = Handover(
            rows=rows, gates=gates,
            row_sel=[keep(f"row_sel{g}", [P, GB4, 1], u32) for g in range(EG)],
            gate_sel=[keep(f"gate_sel{g}", [P, GB4, 1], fp32) for g in range(EG)],
            w_raw=[quarter(w, 0) for w in range(2)],
            picked=[quarter(w, 1).rearrange("p (j d) -> p j d", j=GB4) for w in range(2)],
            w_in=[sem(f"w{w}_in") for w in (1, 2)],
            w_view=[w1.rearrange("e (t p) f -> e p t f", p=P), w2.rearrange("e (t p) d -> e p t d", p=P)],
            sel_done=sem("sel_done"),
            gathered=[sem(f"gathered{g}") for g in range(EG)],
            out_stored=sem("out_stored"))
        banks = [ctx.enter_context(nc.psum_tensor(f"bank{i}", [P, 512], fp32)) for i in range(8)]

        with ExitStack() as mem:
            def sb(name, shape, dt):
                return mem.enter_context(nc.sbuf_tensor(name, shape, dt))

            qstk.append(sb("qstk1", [P, H, T], bf16))
            kstk.append(sb("kstk1", [P, H, T], bf16))
            vaug = [sb(f"vaug{u}", [P, TT, H, 2 * HD], fp32) for u in range(2)]
            probs = [sb(f"probs{u}", [P, 2 * 5 * 512], fp32) for u in range(2)]
            xln = sb("xln", [P, TT, D], fp32)
            xn = sb("xn", [P, TT, D], fp32)
            xt_hi = sb("xt_hi", [P, DT, T], f32r)
            xt_lo = sb("xt_lo", [P, DT, T], f32r)
            rest = [sb(f"rest{u}", [P, T], fp32) for u in range(2)]
            qk_part = [sb(f"qk_part{n}", [P, 4, T], bf16) for n in range(3)]
            yraw = [sb(f"yraw{u}", [P, T], fp32) for u in range(2)]
            ytok = sb("ytok", [P, TT, D], fp32)
            yt_hi = sb("yt_hi", [P, DT, T], f32r)
            yt_lo = sb("yt_lo", [P, DT, T], f32r)
            junk = [sb(f"junk{u}", [P, 512], bf16) for u in range(2)]
            maxrow = [sb(f"maxrow{u}", [2 * GH, T], bf16) for u in range(2)]
            rowmax = [sb(f"rowmax{u}", [P, TT, GH], fp32) for u in range(2)]
            negmax = [sb(f"negmax{u}", [P, TT, SHIFT, GH], bf16) for u in range(2)]
            rden = sb("rden", [P, TT, GH], fp32)
            stats = sb("stats", [P, TT, 6], fp32)
            meanvar = sb("meanvar", [P, TT, 2], fp32)
            vareps = sb("vareps", [P, TT], fp32)
            rstd = sb("rstd", [P, TT], fp32)
            ones_bf = sb("ones_bf", [P, H * T * SHIFT // P], bf16)
            mhalf = sb("mhalf", [P, TT], fp32)
            eps = sb("eps", [P, TT], fp32)
            wqk_hi = sb("wqk_hi", [P, DT, 2 * D], f32r)
            wqk_lo = sb("wqk_lo", [P, DT, 2 * D], f32r)
            wv_hi = sb("wv_hi", [P, DT, D + E], f32r)
            wv_lo = sb("wv_lo", [P, DT, D + E], f32r)
            wo_hi = sb("wo_hi", [P, DT, D], f32r)
            wo_lo = sb("wo_lo", [P, DT, D], f32r)
            vb_all = sb("vb_all", [P, D], fp32)
            ob_all = sb("ob_all", [P, D], fp32)
            rowmask = sb("rowmask", [P, T], fp32)
            colmask = sb("colmask", [P, P], bf16)
            fold_raw = [probs[w][:, 0:DT * H * R].rearrange("p (t h r) -> p t h r", t=DT, h=H) for w in range(2)]
            vw_raw = probs[0][:, 2048:2560].rearrange("p (t d) -> p t d", t=DT)
            ow_raw = probs[1][:, 2048:2560].rearrange("p (t d) -> p t d", t=DT)
            choice_raw = probs[0][0:E, 2560:2560 + D]
            foldb = probs[1][:, 2560:2560 + 2 * D].rearrange("p (w c j) -> p w c j", w=2, c=H // 2)
            fold_t = [[probs[half][:, 3072 + 512 * n:3584 + 512 * n] for half in range(2)] for n in range(2 * DT)]

            dve_past, sp_past = sem("dve_past"), sem("sp_past")
            fold_a_in = [sem(f"fold_a_in{n}") for n in range(2 * DT)]
            fold_b_in = sem("fold_b_in")
            weights_in = sem("weights_in")
            ident_done = sem("ident_done")
            ones_done = sem("ones_done")
            ones_in = sem("ones_in")
            consts = sem("consts")
            zeroed = sem("zeroed")
            foldb_zero = sem("foldb_zero")
            x_in = sem("x_in")
            stats_done = sem("stats_done")
            mv_done = sem("mv_done")
            vareps_done = sem("vareps_done")
            rstd_done = sem("rstd_done")
            xn_done = sem("xn_done")
            xn_stored = sem("xn_stored")
            shared_ready = [sem(f"shared_ready{u}") for u in range(2)]
            shared_done = [sem(f"shared_done{u}") for u in range(2)]
            hi_done = sem("hi_done")
            mid_done = sem("mid_done")
            lo_done = sem("lo_done")
            stacked = [sem(f"stacked{u}") for u in range(2)]
            logit_done = sem("logit_done")
            score_ready = sem("score_ready")
            score_done = sem("score_done")
            neghi_done = sem("neghi_done")
            negmax_done = sem("negmax_done")
            max_in = [sem(f"max_in{u}") for u in range(2)]
            scoret_ready = sem("scoret_ready")
            exp_done = sem("exp_done")
            pv_ready = sem("pv_ready")
            yraw_done = sem("yraw_done")
            rden_done = sem("rden_done")
            xres_in = sem("xres_in")
            xres_done = sem("xres_done")
            out_stored = moe.out_stored
            gate_step = sem("gate_step")
            gate_exp = sem("gate_exp")
            ids = sem("ids")

            xn_flat, xln_flat = (t[:].rearrange("p t d -> p (t d)") for t in (xn, xln))
            gate = xn_flat[:, 0:T].rearrange("p (t r) -> p t r", t=TT)
            top, top_row = xn_flat[:, T:T + CAP], xn_flat[:, T + CAP:T + 2 * CAP]
            top_at = xn_flat[:, T + 2 * CAP:T + 3 * CAP].bitcast(u32)
            gsum = xn_flat[:, T + 3 * CAP:T + 3 * CAP + TT * B]
            ranked = [xln_flat[:, T * u:T * u + T] for u in range(2)]
            first_i = [sb(f"first_i{u}", [P, 1], i32) for u in range(3)]
            first = sb("first", [P, 1], fp32)
            GATED = 8

            SCORE, SCORET, Y, SHARED = banks[0:3], banks[3:5], banks[5], banks[6:8]
            FIRST, PER_PAIR = UN * 3, UN * GB * 2

            def score_bank(u):
                return (u if u < FIRST else (u - FIRST) % PER_PAIR) % 3

            def score_back(u):
                return next(d for d in range(1, 6) if score_bank(u - d) == score_bank(u))

            N_CONST = 5
            STACK_DMAS = 16 * 2 * len(TERMS)
            N_WEIGHTS = 16 * 5

            def program(eng, steps_fn):
                same = lambda value, per_pair: value
                steps_fn(prologue_steps() + pair_steps(0), same)
                with eng.Fori(1, PAIRS - 1) as i:
                    steps_fn(pair_steps(1), lambda value, per_pair: i * per_pair + (value - per_pair))
                steps_fn(pair_steps(PAIRS - 1) + epilogue_steps(), same)

            def bank_of(step):
                return unit_of[step] % 2

            def filled(step, at):
                return at(unit_of[step] // 2 + 1, U_PAIR // 2)

            def emptied(step, at):
                return at(unit_of[step] // 2 + 1, U_PAIR // 2)

            def split(step, at):
                return at(split_of[step] + 1, S_PAIR)

            block = mem.enter_context(nc.Block())

            @block.sync
            def _(sp):
                def ones():
                    sp.wait_ge(ones_done, 1)
                    for u in range(2):
                        sp.dma_start(kstk[u][KS:KS + SHIFT, :, :], ones_bf[:]).then_inc(ones_in, 16)

                def steps(todo, at):
                    for step in todo:
                        kind, n, k = step
                        if kind == "xload":
                            if n >= 1:
                                sp.wait_ge(xn_done, at(n, 2))
                                sp.sem_inc(sp_past, 1)
                            sp.dma_start(xln[:], x_v[at(n, 2)]).then_inc(x_in, 16)
                            if n == 0:
                                ones()
                        elif kind == "lnapply":
                            sp.wait_ge(xn_done, at(n + 1, 2))
                            sp.sem_inc(sp_past, 1)
                            sp.dma_start(xn_v[at(n, 2)], xn[:]).then_inc(xn_stored, 16)
                        elif kind == "mid" and k % 2 == 1:
                            if n >= 2 and k == 1:
                                sp.wait_ge(scoret_ready, at(UN * GB * (n - 1), 8 * UN))
                                sp.sem_inc(sp_past, 1)
                            sp.wait_ge(lo_done, at(GB * n + k + 1, 2 * GB))
                            side = k // 2
                            stk = (qstk, kstk)[side][n % 2]
                            for t, term in enumerate(TERMS):
                                sp.dma_start(stk[HD * t:HD * t + HD, :, :],
                                             qk_part[term[side]][:, 2 * side:2 * side + 2, :]).then_inc(stacked[n % 2], 16)
                        elif kind == "maxt":
                            sp.wait_ge(shared_done[bank_of(step)], emptied(step, at))
                            sp.sem_inc(sp_past, 1)
                            b, g = divmod(n, GB)
                            for s in range(SHIFT):
                                sp.dma_start(qstk[b % 2][KS + s:KS + s + 1, GH * g:GH * g + GH, :],
                                             maxrow[n % 2][GH * s:GH * s + GH, :]).then_inc(max_in[n % 2], 16)
                        elif kind == "xres":
                            if n >= 1:
                                sp.wait_ge(out_stored, at(16 * n, 32))
                                sp.sem_inc(sp_past, 1)
                            sp.dma_start(xres[:], x_v[at(n, 2)]).then_inc(xres_in, 16)
                        elif kind == "o" and k == TT - 1:
                            sp.wait_ge(shared_done[bank_of(step)], emptied(step, at))
                            sp.sem_inc(sp_past, 1)
                            sp.wait_ge(shared_done[bank_of(("o", n, TT - 2))], emptied(("o", n, TT - 2), at))
                            sp.sem_inc(sp_past, 1)
                            sp.dma_start(out_v[at(n, 2)], xres[:]).then_inc(out_stored, 16)

                        elif kind == "w_load":
                            sp.wait_ge(scoret_ready, UN * GB * (B - 1))
                            for w in range(2):
                                sp.dma_start(moe.w_raw[w], moe.w_view[w][0]).then_inc(moe.w_in[w], 16)

                program(sp, steps)

            @block.gpsimd
            def _(pool):
                nc.gpsimd.memset(mhalf[:], -0.5).then_inc(consts, 1)
                nc.gpsimd.memset(eps[:], EPS).then_inc(consts, 1)
                nc.gpsimd.memset(ident[:], 0.0).then_inc(zeroed, 1)
                nc.gpsimd.memset(ident_bf[:], 0.0).then_inc(zeroed, 1)
                nc.gpsimd.memset(colmask[:], 0.0).then_inc(zeroed, 1)
                pool.wait_ge(zeroed, 1)
                nc.gpsimd.affine_select(out=ident[:], in_=ident[:], compare_op=ALU.not_equal, fill=1.0, base=0,
                                        pattern=[[-1, P]], channel_multiplier=1).then_inc(ident_done, 1)
                nc.gpsimd.memset(rowmask[:], 0.0).then_inc(zeroed, 1)
                pool.wait_ge(zeroed, 4)
                nc.gpsimd.affine_select(out=ident_bf[:], in_=ident_bf[:], compare_op=ALU.not_equal, fill=1.0, base=0,
                                        pattern=[[-1, P]], channel_multiplier=1).then_inc(consts, 1)
                nc.gpsimd.affine_select(out=colmask[:], in_=colmask[:], compare_op=ALU.is_ge, fill=NEG, base=0,
                                        pattern=[[-1, P]], channel_multiplier=1).then_inc(consts, 1)
                nc.gpsimd.affine_select(out=rowmask[:, T - P:T], in_=rowmask[:, T - P:T], compare_op=ALU.is_ge,
                                        fill=NEG, base=0, pattern=[[-1, P]], channel_multiplier=1).then_inc(consts, 1)
                nc.gpsimd.iota(first_i[0][:], pattern=[[0, 1]], base=0, channel_multiplier=1).then_inc(ids, 1)

                def steps(todo, at):
                    for step in todo:
                        kind, n, k = step
                        if kind == "gather":
                            pool.wait_ge(moe.sel_done, n + 1)
                            pool.wait_ge(xn_stored, 16 * B)
                            gather(nc, moe, xn_dram, n)
                        elif kind == "lnstat" and k == 1:
                            pool.wait_ge(mv_done, at(n + 1, 2))
                            if n >= 1:
                                pool.wait_ge(xn_done, at(n, 2))
                            nc.gpsimd.tensor_tensor(vareps[:], meanvar[:, :, 1], eps[:], ALU.add).then_inc(vareps_done, 1)
                            pool.wait_ge(vareps_done, at(n + 1, 2))
                            nc.gpsimd.tensor_tensor(rstd[:], vareps[:], mhalf[:], ALU.pow).then_inc(rstd_done, 1)
                        elif kind == "mid":
                            pool.wait_ge(mid_done, at(GB * n + k + 1, 2 * GB))
                            if n >= 1:
                                pool.wait_ge(stacked[(n - 1) % 2], at(STACK_DMAS * ((n - 1) // 2 + 1), STACK_DMAS))
                            nc.gpsimd.tensor_tensor(qk_part[2][:, k, :], rest[k % 2][:], qk_part[1][:, k, :],
                                                    ALU.subtract).then_inc(lo_done, 1)
                        elif kind == "xres":
                            pool.wait_ge(xres_in, at(16 * (n + 1), 32))
                            if n == 0:
                                pool.wait_ge(weights_in, N_WEIGHTS)
                            nc.gpsimd.tensor_tensor(xres[:], xres[:], ob_all[:].unsqueeze(1).to_broadcast([P, TT, D]),
                                                    ALU.add).then_inc(xres_done, 1)

                program(pool, steps)

            @block.scalar
            def _(act):
                act.wait_ge(foldb_zero, 1)
                for w, (raw_a, raw_b) in enumerate(((q_a, q_b), (k_a, k_b))):
                    for dt in range(DT):
                        act.dma_start(fold_raw[w][:, dt, :, :],
                                      raw_a[:, P * dt:P * dt + P, :].rearrange("h p r -> p h r"))\
                            .then_inc(fold_a_in[DT * w + dt], 16)
                    for odd in range(2):
                        act.dma_start(foldb[R * odd:R * odd + R, w, :, HD * odd:HD * odd + HD],
                                      raw_b.rearrange("(c two) r j -> two r c j", two=2)[odd]).then_inc(fold_b_in, 16)
                act.dma_start(vw_raw, v_w.rearrange("(t p) d -> p t d", p=P)).then_inc(weights_in, 16)
                act.dma_start(choice_raw, choice_w).then_inc(weights_in, 16)
                act.dma_start(vb_all[:], v_b.partition_broadcast(P)).then_inc(weights_in, 16)
                act.dma_start(ow_raw, o_w.rearrange("(t p) d -> p t d", p=P)).then_inc(weights_in, 16)
                act.dma_start(ob_all[:], o_b.partition_broadcast(P)).then_inc(weights_in, 16)

                def steps(todo, at):
                    for step in todo:
                        kind, n, k = step
                        if step in unit_of:
                            p, src = bank_of(step), SHARED[bank_of(step)]
                        if kind == "gate_exp":
                            act.wait_ge(gate_step, 2)
                            nc.scalar.activation(gate, gate, ACT.Exp).then_inc(gate_exp, 1)
                        elif kind == "rankt":
                            act.wait_ge(shared_ready[p], filled(step, at))
                            act.wait_ge(xn_done, B)
                            nc.scalar.activation(ranked[0], src[:], ACT.Copy).then_inc(shared_done[p], 1)
                        elif kind == "foldt" and k == 0:
                            act.wait_ge(shared_ready[p], filled(step, at))
                            nc.scalar.activation(fold_t[n][0], src[:], ACT.Copy).then_inc(shared_done[p], 1)
                        elif kind == "fold":
                            act.wait_ge(shared_ready[p], filled(step, at))
                            w, dt = divmod(n, DT)
                            nc.scalar.activation(
                                wqk_hi[:, dt, D * w:D * w + D].rearrange("p (m j h) -> p m h j", m=2, h=8),
                                src[:, 0:D].rearrange("p (h m j) -> p m h j", m=2, h=8), ACT.Copy).then_inc(hi_done, 1)
                        elif kind == "wv":
                            act.wait_ge(shared_ready[p], filled(step, at))
                            nc.scalar.activation(wv_hi[:, n, :], src[:, 0:D + E], ACT.Copy).then_inc(hi_done, 1)
                        elif kind == "wo":
                            act.wait_ge(shared_ready[p], filled(step, at))
                            nc.scalar.activation(wo_hi[:, n, :], src[:, 0:D], ACT.Copy).then_inc(hi_done, 1)
                        elif kind == "xt":
                            act.wait_ge(shared_ready[p], filled(step, at))
                            nc.scalar.activation(xt_hi[:, k, :], src[:], ACT.Copy).then_inc(hi_done, 1)
                        elif kind == "yt":
                            act.wait_ge(shared_ready[p], filled(step, at))
                            nc.scalar.activation(yt_hi[:, k, :], src[:], ACT.Copy).then_inc(hi_done, 1)
                        elif kind == "qk":
                            act.wait_ge(shared_ready[p], filled(step, at))
                            if n >= 1 and k == 0:
                                act.wait_ge(stacked[(n - 1) % 2], at(STACK_DMAS * ((n - 1) // 2 + 1), STACK_DMAS))
                            nc.scalar.activation(qk_part[0][:, k, :], src[:], ACT.Copy).then_inc(hi_done, 1)
                        elif kind == "mid":
                            qk = ("qk", n, k)
                            act.wait_ge(shared_done[bank_of(qk)], emptied(qk, at))
                            nc.scalar.activation(qk_part[1][:, k, :], rest[k % 2][:], ACT.Copy).then_inc(mid_done, 1)
                        elif kind == "v":
                            act.wait_ge(shared_ready[p], filled(step, at))
                            nc.scalar.activation(logits[:, k, at(n, 2), :], src[:, D:D + E], ACT.Copy).then_inc(logit_done, 1)
                        elif kind == "maxt":
                            act.wait_ge(shared_ready[p], filled(step, at))
                            if n >= 2:
                                act.wait_ge(max_in[n % 2], at(32 * (n // 2), 128))
                            nc.scalar.activation(maxrow[n % 2][:], src[:].bitcast(bf16)[0:2 * GH, 0:T], ACT.Copy)\
                                .then_inc(shared_done[p], 1)
                        elif kind == "scoret":
                            act.wait_ge(scoret_ready, at(UN * n + k + 1, 8 * UN))
                            if k == 0 and n >= 2:
                                act.wait_ge(pv_ready, at(n - 1, 8))
                            nc.scalar.activation(probs[n % 2][:, 512 * k:512 * k + 512], SCORET[k % 2][:], ACT.Exp,
                                                 scale=SCALE).then_inc(exp_done, 1)
                        elif kind == "pv" and k == TT - 1:
                            act.wait_ge(pv_ready, at(n + 1, 8))
                            nc.scalar.activation(yraw[n % 2][:], Y[:], ACT.Copy).then_inc(yraw_done, 1)

                program(act, steps)

            @block.vector
            def _(dve):
                nc.vector.memset(foldb, 0.0).then_inc(foldb_zero, 1)
                nc.vector.memset(ones_bf[:], 1.0).then_inc(ones_done, 1)
                for u in range(2):
                    nc.vector.memset(vaug[u][:, :, :, HD:2 * HD], 1.0).then_inc(ones_done, 1)
                log_v = logits[:].rearrange("p t b e -> p (t b) e")
                gate_e = gate.rearrange("p t (b e) -> p (t b) e", e=E)
                over_e = gsum.unsqueeze(2).to_broadcast([P, TT * B, E])
                by_be = lambda t: t[:].rearrange("p b e -> p (b e)")

                def take_low(step, at, low, whole, high):
                    p = bank_of(step)
                    dve.wait_ge(hi_done, split(step, at))
                    nc.vector.tensor_tensor(low, whole, high, ALU.subtract).then_inc(shared_done[p], 1)

                def steps(todo, at):
                    for step in todo:
                        kind, n, k = step
                        if step in unit_of:
                            p, src = bank_of(step), SHARED[bank_of(step)]
                        if kind == "gate_max":
                            dve.wait_ge(logit_done, B * TT)
                            dve.wait_ge(xn_stored, 16 * B)
                            prev = ("xt", B - 1, 1)
                            dve.wait_ge(shared_ready[bank_of(prev)], filled(prev, at))
                            nc.vector.reduce_max(gsum, log_v, AX.X).then_inc(gate_step, 1)
                            dve.wait_ge(gate_step, 1)
                            nc.vector.tensor_tensor(gate_e, log_v, over_e, ALU.subtract).then_inc(gate_step, 1)
                        elif kind == "gate_norm":
                            dve.wait_ge(gate_exp, 1)
                            nc.vector.reduce_sum(gsum, gate_e, AX.X).then_inc(gate_step, 1)
                            dve.wait_ge(gate_step, 3)
                            nc.vector.reciprocal(gsum, gsum).then_inc(gate_step, 1)
                            dve.wait_ge(gate_step, 4)
                            nc.vector.tensor_tensor(gate_e, gate_e, over_e, ALU.mult).then_inc(gate_step, 1)
                            dve.wait_ge(ids, 1)
                            nc.vector.tensor_single_scalar(first_i[1][:], first_i[0][:], E.bit_length() - 1,
                                                           ALU.arith_shift_right).then_inc(gate_step, 1)
                            dve.wait_ge(gate_step, 6)
                            nc.vector.tensor_single_scalar(first_i[2][:], first_i[1][:], T.bit_length() - 1,
                                                           ALU.logical_shift_left).then_inc(gate_step, 1)
                            dve.wait_ge(gate_step, 7)
                            nc.vector.tensor_copy(first[:], first_i[2][:]).then_inc(gate_step, 1)
                        elif kind == "rank":
                            if n == 0:
                                prev = ("rankt", 0, 0)
                                dve.wait_ge(shared_done[bank_of(prev)], emptied(prev, at))
                            dve.wait_ge(gate_step, GATED + n)
                            r, op = divmod(n, 3)
                            a, z, eight = ranked[r % 2], ranked[(r + 1) % 2], slice(8 * r, 8 * r + 8)
                            if op == 0:
                                last = nc.vector.max(top[:, eight], a)
                            elif op == 1:
                                last = nc.vector.max_index(top_at[:, eight], top[:, eight], a)
                            else:
                                last = nc.vector.match_replace(z, top[:, eight], a, -1.0)
                            last.then_inc(gate_step, 1)
                        elif kind == "rows":
                            dve.wait_ge(gate_step, GATED + RANK_OPS)
                            nc.vector.tensor_copy(top_row, top_at).then_inc(gate_step, 1)
                            dve.wait_ge(gate_step, GATED + RANK_OPS + 1)
                            nc.vector.tensor_scalar(top_row, top_row, first[:], None, ALU.add).then_inc(gate_step, 1)
                        elif kind == "rowst":
                            dve.wait_ge(shared_ready[p], filled(step, at))
                            nc.vector.tensor_copy(by_be(rows), src[:, 0:P]).then_inc(gate_step, 1)
                            nc.vector.tensor_copy(by_be(gates), src[:, P:2 * P]).then_inc(shared_done[p], 1)
                        elif kind == "gather":
                            if n == 0:
                                prev = ("rowst", 0, 0)
                                dve.wait_ge(gate_step, GATED + RANK_OPS + 3)
                                dve.wait_ge(shared_done[bank_of(prev)], emptied(prev, at))
                            select(nc, moe, n, 0)
                        elif kind == "lnstat":
                            dve.wait_ge(x_in, at(16 * (n + 1), 32))
                            for tt in (2 * k, 2 * k + 1):
                                last = nc.vector.bn_stats(stats[:, tt, :], xln[:, tt, :])
                            last.then_inc(stats_done, 1)
                            if k == 1:
                                dve.wait_ge(stats_done, at(2 * (n + 1), 4))
                                dve.sem_inc(dve_past, 1)
                                for tt in range(TT):
                                    last = nc.vector.bn_aggr(meanvar[:, tt, :], stats[:, tt, :])
                                last.then_inc(mv_done, 1)
                        elif kind == "lnapply":
                            dve.wait_ge(rstd_done, at(n + 1, 2))
                            if n >= 1:
                                dve.wait_ge(xn_stored, at(16 * n, 32))
                                prev = ("xt", n - 1, 1)
                                dve.wait_ge(shared_ready[bank_of(prev)], filled(prev, at))
                            for tt in range(TT):
                                last = nc.vector.tensor_scalar(xn[:, tt, :], xln[:, tt, :], meanvar[:, tt, 0:1],
                                                               rstd[:, tt:tt + 1], ALU.subtract, ALU.mult)
                            last.then_inc(xn_done, 1)
                        elif kind == "foldt" and k == 1:
                            dve.wait_ge(shared_ready[p], filled(step, at))
                            nc.vector.tensor_copy(fold_t[n][1], src[:]).then_inc(shared_done[p], 1)
                        elif kind == "fold":
                            w, dt = divmod(n, DT)
                            view = "p (m j h) -> p m h j"
                            take_low(step, at, wqk_lo[:, dt, D * w:D * w + D].rearrange(view, m=2, h=8),
                                     src[:, 0:D].rearrange("p (h m j) -> p m h j", m=2, h=8),
                                     wqk_hi[:, dt, D * w:D * w + D].rearrange(view, m=2, h=8))
                        elif kind == "wv":
                            take_low(step, at, wv_lo[:, n, :], src[:, 0:D + E], wv_hi[:, n, :])
                        elif kind == "wo":
                            take_low(step, at, wo_lo[:, n, :], src[:, 0:D], wo_hi[:, n, :])
                        elif kind == "xt":
                            take_low(step, at, xt_lo[:, k, :], src[:], xt_hi[:, k, :])
                        elif kind == "yt":
                            take_low(step, at, yt_lo[:, k, :], src[:], yt_hi[:, k, :])
                        elif kind == "qk":
                            if 4 * n + k >= 2:
                                dve.wait_ge(lo_done, at(4 * n + k - 1, 8))
                            take_low(step, at, rest[k % 2][:], src[:], qk_part[0][:, k, :])
                        elif kind == "v":
                            dve.wait_ge(logit_done, at(4 * n + k + 1, 8))
                            nc.vector.tensor_tensor(vaug[n % 2][:, k, :, 0:HD],
                                                    src[:, 0:D].rearrange("p (h j) -> p h j", h=H),
                                                    vb_all[:].rearrange("p (h j) -> p h j", h=H), ALU.add)\
                                .then_inc(shared_done[p], 1)
                        elif kind == "score":
                            u = UN * n + k
                            if u == 0:
                                dve.wait_ge(consts, N_CONST)
                            dve.wait_ge(score_ready, at(u + 1, 8 * UN))
                            if u >= 2:
                                dve.wait_ge(score_done, at(u - 1, 8 * UN))
                            if k == 0 and n >= 2:
                                dve.wait_ge(negmax_done, at(n - 1, 8))
                            dve.sem_inc(dve_past, 1)
                            for h, i, col, width in unit_parts(k, False):
                                last = nc.vector.tensor_tensor_reduce(
                                    out=junk[k % 2][:, col:col + width], in0=SCORE[score_bank(UN * n + k)][:, col:col + width],
                                    in1=rowmask[:, T - width:T], scale=1.0, scalar=-3e38, op0=ALU.add, op1=ALU.max,
                                    accum_out=rowmax[n % 2][:, i, h:h + 1])
                            last.then_inc(score_done, 1)
                            if k == UN - 1:
                                if n >= 2:
                                    prev = ("maxt", n - 2, 0)
                                    dve.wait_ge(shared_ready[bank_of(prev)], filled(prev, at))
                                dve.wait_ge(score_done, at(u + 1, 8 * UN))
                                nc.vector.tensor_scalar(negmax[n % 2][:, :, 0, :], rowmax[n % 2][:], -1.0, None, ALU.mult)\
                                    .then_inc(neghi_done, 1)
                                dve.wait_ge(neghi_done, at(n + 1, 8))
                                nc.vector.scalar_tensor_tensor(out=negmax[n % 2][:, :, 1, :], in0=rowmax[n % 2][:],
                                                               scalar=-1.0, in1=negmax[n % 2][:, :, 0, :],
                                                               op0=ALU.mult, op1=ALU.subtract).then_inc(negmax_done, 1)
                        elif kind == "ytr":
                            dve.wait_ge(shared_ready[p], filled(step, at))
                            y4 = src[:].rearrange("p (q h c) -> p q h c", q=TT, h=GH)
                            if n >= 1:
                                prev = ("ytr", n - 1, 0)
                                dve.wait_ge(shared_done[bank_of(prev)], emptied(prev, at))
                            nc.vector.reciprocal(rden[:], y4[:, :, :, HD]).then_inc(rden_done, 1)
                            dve.wait_ge(rden_done, at(n + 1, 8))
                            if n % GB == 0 and n >= GB:
                                prev = ("yt", n // GB - 1, 1)
                                dve.wait_ge(shared_ready[bank_of(prev)], filled(prev, at))
                            g = n % GB
                            nc.vector.tensor_tensor(
                                ytok[:, :, GH * HD * g:GH * HD * (g + 1)].rearrange("p q (h c) -> p q h c", h=GH),
                                y4[:, :, :, 0:HD], rden[:].unsqueeze(3).to_broadcast([P, TT, GH, HD]), ALU.mult)\
                                .then_inc(shared_done[p], 1)
                        elif kind == "o":
                            dve.wait_ge(shared_ready[p], filled(step, at))
                            dve.wait_ge(xres_done, at(n + 1, 2))
                            nc.vector.tensor_tensor(xres[:, k, :], src[:, 0:D], xres[:, k, :], ALU.add).then_inc(shared_done[p], 1)

                program(dve, steps)

            @block.tensor
            def _(pe):
                pe.wait_ge(ident_done, 1)

                def three_passes(dst, left_hi, left_lo, right_hi, right_lo):
                    todo = [(left(dt), right(dt)) for dt in range(DT)
                            for left, right in ((left_hi, right_hi), (left_hi, right_lo), (left_lo, right_hi))]
                    for m, (a, b) in enumerate(todo):
                        last = nc.tensor.matmul(dst, a, b, start=m == 0, stop=m == len(todo) - 1)
                    return last

                def qk_passes(dst, mt, dt):
                    cols = slice(P * mt, P * mt + P)
                    for m, (a, b) in enumerate(((wqk_hi, xt_hi), (wqk_hi, xt_lo), (wqk_lo, xt_hi))):
                        last = nc.tensor.matmul(dst, a[:, dt, cols], b[:, dt, :],
                                                start=dt == 0 and m == 0, stop=dt == DT - 1 and m == 2)
                    return last

                def await_units(step, sources, at):
                    other = [s for s in sources if bank_of(s) != bank_of(step)] if step in unit_of else sources
                    for u in range(2):
                        mine = [s for s in other if bank_of(s) == u]
                        if mine:
                            pe.wait_ge(shared_done[u], emptied(max(mine, key=unit_of.get), at))

                def steps(todo, at):
                    for step in todo:
                        kind, n, k = step
                        if kind == "qk_first":
                            step = ("qk", n, k)
                        if step in unit_of:
                            p, dst = bank_of(step), SHARED[bank_of(step)]
                            if unit_of[step] >= 2 and kind != "qk":
                                pe.wait_ge(shared_done[p], at(unit_of[step] // 2, U_PAIR // 2))
                        if kind == "rankt":
                            pe.wait_ge(gate_step, 5)
                            for tt in range(TT):
                                last = nc.tensor.transpose(dst[:, P * tt:P * tt + P], gate[:, tt, :], ident[:])
                            last.then_inc(shared_ready[p], 1)
                        elif kind == "rowst":
                            pe.wait_ge(gate_step, GATED + RANK_OPS + 2)
                            nc.tensor.transpose(dst[:, 0:P], top_row, ident[:])
                            nc.tensor.transpose(dst[:, P:2 * P], top, ident[:]).then_inc(shared_ready[p], 1)
                        elif kind == "foldt":
                            pe.wait_ge(fold_a_in[n], 16)
                            w, dt = divmod(n, DT)
                            for c in range(4):
                                h = 2 * (4 * k + c)
                                last = nc.tensor.transpose(dst[:, P * c:P * c + P],
                                                           fold_raw[w][:, dt, h:h + 2, :].rearrange("p h r -> p (h r)"), ident[:])
                            last.then_inc(shared_ready[p], 1)
                        elif kind == "fold":
                            if n == 0:
                                pe.wait_ge(fold_b_in, 16 * 4)
                            await_units(step, [("foldt", n, half) for half in range(2)], at)
                            for c in range(H // 2):
                                last = nc.tensor.matmul(dst[:, 2 * HD * c:2 * HD * c + 2 * HD],
                                                        fold_t[n][c // 4][:, P * (c % 4):P * (c % 4) + P],
                                                        foldb[:, n // DT, c, :], start=True, stop=True)
                            last.then_inc(shared_ready[p], 1)
                        elif kind == "wv":
                            pe.wait_ge(weights_in, N_WEIGHTS)
                            for t in range(DT):
                                nc.tensor.transpose(dst[:, P * t:P * t + P], vw_raw[:, t, P * n:P * n + P], ident[:])
                            nc.tensor.transpose(dst[:, D:D + E], choice_raw[:, P * n:P * n + P], ident[0:E, 0:E])\
                                .then_inc(shared_ready[p], 1)
                        elif kind == "wo":
                            for t in range(DT):
                                last = nc.tensor.transpose(dst[:, P * t:P * t + P], ow_raw[:, t, P * n:P * n + P], ident[:])
                            last.then_inc(shared_ready[p], 1)
                        elif kind == "xt":
                            pe.wait_ge(xn_done, at(n + 1, 2))
                            for tt in range(TT):
                                last = nc.tensor.transpose(dst[:, P * tt:P * tt + P], xn[:, tt, P * k:P * k + P], ident[:])
                            last.then_inc(shared_ready[p], 1)
                        elif kind == "qk_first":
                            await_units(step, [("xt", n, dt) for dt in range(DT)]
                                        + [("fold", w, 0) for w in range(2 * DT) if n == 0], at)
                            qk_passes(dst[:], k, 0)
                        elif kind == "qk":
                            qk_passes(dst[:], k, 1).then_inc(shared_ready[p], 1)
                        elif kind == "v":
                            await_units(step, [("wv", dt, 0) for dt in range(DT) if n == 0], at)
                            rows = slice(P * k, P * k + P)
                            three_passes(dst[:, 0:D + E], lambda dt: xt_hi[:, dt, rows], lambda dt: xt_lo[:, dt, rows],
                                         lambda dt: wv_hi[:, dt, :], lambda dt: wv_lo[:, dt, :]).then_inc(shared_ready[p], 1)
                        elif kind == "score":
                            u, (b, g) = UN * n + k, divmod(n, GB)
                            if u >= 3:
                                pe.wait_ge(score_done, at(u - score_back(u) + 1, 8 * UN))
                            if g == 0 and k == 0:
                                pe.wait_ge(stacked[b % 2], at(STACK_DMAS * (b // 2 + 1), STACK_DMAS))
                            for h, i, col, width in unit_parts(k, False):
                                last = nc.tensor.matmul(SCORE[score_bank(UN * n + k)][:, col:col + width],
                                                        qstk[b % 2][0:KS, GH * g + h, P * i:P * i + P],
                                                        kstk[b % 2][0:KS, GH * g + h, 0:width], start=True, stop=True)
                            last.then_inc(score_ready, 1)
                        elif kind == "maxt":
                            pe.wait_ge(negmax_done, at(n + 1, 8))
                            if n == 0:
                                pe.wait_ge(consts, N_CONST)
                            for i in range(TT):
                                last = nc.tensor.transpose(dst[:].bitcast(bf16)[0:2 * GH, P * i:P * i + P],
                                                           negmax[n % 2][:, i, :, :].rearrange("p s h -> p (s h)"), ident_bf[:])
                            last.then_inc(shared_ready[p], 1)
                        elif kind == "scoret":
                            u, (b, g) = UN * n + k, divmod(n, GB)
                            if u >= 2:
                                pe.wait_ge(exp_done, at(u - 1, 8 * UN))
                            if u == 0:
                                pe.wait_ge(ones_in, 16 * 2)
                            if k == 0:
                                pe.wait_ge(max_in[n % 2], at(32 * (n // 2 + 1), 128))
                            for h, j, col, width in unit_parts(k, True):
                                nc.tensor.matmul(SCORET[k % 2][:, col:col + width],
                                                 kstk[b % 2][0:KS + SHIFT, GH * g + h, P * j:P * j + P],
                                                 qstk[b % 2][0:KS + SHIFT, GH * g + h, P * j:T], start=True, stop=False)
                                last = nc.tensor.matmul(SCORET[k % 2][:, col:col + P], colmask[:], ident_bf[:],
                                                        start=False, stop=True)
                            last.then_inc(scoret_ready, 1)
                        elif kind == "pv":
                            b, g = divmod(n, GB)
                            if k == 0:
                                pe.wait_ge(exp_done, at(UN * (n + 1), 8 * UN))
                                if n == 0:
                                    pe.wait_ge(ones_done, 3)
                                if g == 0:
                                    await_units(step, [("v", b, tt) for tt in range(TT)], at)
                                if n >= 1:
                                    pe.wait_ge(yraw_done, at(n, 8))
                            where = {(h, j): (512 * t + col, width) for t in range(UN)
                                     for h, j, col, width in unit_parts(t, True)}
                            for h in range(GH):
                                col, width = where[h, k]
                                last = nc.tensor.matmul(Y[2 * HD * h:2 * HD * h + 2 * HD, P * k:T],
                                                        vaug[b % 2][:, k, GH * g + h, :],
                                                        probs[n % 2][:, col:col + width],
                                                        start=k == 0, stop=k == TT - 1)
                            if k == TT - 1:
                                last.then_inc(pv_ready, 1)
                        elif kind == "ytr":
                            pe.wait_ge(yraw_done, at(n + 1, 8))
                            for i in range(TT):
                                last = nc.tensor.transpose(dst[:, P * i:P * i + P], yraw[n % 2][:, P * i:P * i + P], ident[:])
                            last.then_inc(shared_ready[p], 1)
                        elif kind == "yt":
                            await_units(step, [("ytr", GB * n + g, 0) for g in range(GB)], at)
                            for tt in range(TT):
                                last = nc.tensor.transpose(dst[:, P * tt:P * tt + P], ytok[:, tt, P * k:P * k + P], ident[:])
                            last.then_inc(shared_ready[p], 1)
                        elif kind == "o":
                            await_units(step, [("yt", n, dt) for dt in range(DT)]
                                        + [("wo", dt, 0) for dt in range(DT) if n == 0], at)
                            rows = slice(P * k, P * k + P)
                            three_passes(dst[:, 0:D], lambda dt: yt_hi[:, dt, rows], lambda dt: yt_lo[:, dt, rows],
                                         lambda dt: wo_hi[:, dt, :], lambda dt: wo_lo[:, dt, :]).then_inc(shared_ready[p], 1)

                program(pe, steps)

        experts(nc, sem, ident, banks, moe, xn_dram, out_rows)


def expert_steps(e):
    out = []
    for grp in range(EG):
        n = EG * e + grp
        out += [("h", n, ft) for ft in range(FT)]
        if grp == EG - 1 and e + 1 < E:
            out.append(("w", e + 1, 0))
        if n + 1 < E * EG:
            out += [("pick", n + 1, dt) for dt in range(DT)]
        if n + 2 < E * EG:
            out.append(("gather", n + 2, 0))
        if n >= 1:
            out += [("down", n - 1, j) for j in range(GB4 // 2)]
        if grp == 0 and e >= 1:
            out.append(("w", e, 1))
    return out + [("down", n, j) for j in range(GB4 // 2) if e == E - 1]


def gather(nc, moe, xn_dram, n):
    grp = n % EG
    for j in range(GB4):
        nc.gpsimd.indirect_dma_start(
            out=moe.picked[n % 2][:, j, :], out_offset=None, in_=xn_dram,
            in_offset=bass.IndirectOffsetOnAxis(ap=moe.row_sel[grp][:, j, :], axis=0)).then_inc(moe.gathered[grp], 16)


def select(nc, moe, n, e):
    grp = n % EG
    of = slice(GB4 * grp, GB4 * grp + GB4)
    nc.vector.tensor_copy(moe.gate_sel[grp][:], moe.gates[:, of, bass.ds(e, 1)])
    nc.vector.tensor_copy(moe.row_sel[grp][:], moe.rows[:, of, bass.ds(e, 1)]).then_inc(moe.sel_done, 1)


def experts(nc, sem, ident, banks, moe, xn_dram, out_rows):
    fp32, f32r = mybir.dt.float32, mybir.dt.float32r
    ALU, ACT = mybir.AluOpType, mybir.ActivationFunctionType
    assert B * E == P and CAP == P
    start_steps = [("gather", 1, 0), ("w", 0, 0), ("pick", 0, 0), ("pick", 0, 1), ("w", 0, 1)]
    row_sel, gate_sel, picked, gathered, sel_done = moe.row_sel, moe.gate_sel, moe.picked, moe.gathered, moe.sel_done
    with ExitStack() as mem:
        def sb(name, shape, dt):
            return mem.enter_context(nc.sbuf_tensor(name, shape, dt))

        w_hi = [sb(f"w{w}_hi", [P, DT * F], f32r) for w in (1, 2)]
        w_lo = [sb(f"w{w}_lo", [P, DT * F], f32r) for w in (1, 2)]
        w1_hi, w1_lo = (t[0][:].rearrange("p (t f) -> p t f", t=DT) for t in (w_hi, w_lo))
        w2_hi, w2_lo = (t[1][:].rearrange("p (t d) -> p t d", t=FT) for t in (w_hi, w_lo))
        pt_hi, pt_lo = sb("pt_hi", [P, DT, T], f32r), sb("pt_lo", [P, DT, T], f32r)
        hid = [sb(f"hid{u}", [P, T], fp32) for u in range(2)]
        hid_hi = [sb(f"hid_hi{u}", [P, FT, T], f32r) for u in range(2)]
        hid_lo = [sb(f"hid_lo{u}", [P, FT, T], f32r) for u in range(2)]
        mixed = [sb(f"mixed{u}", [P, GB4, D], fp32) for u in range(2)]
        PICK, UP, DOWN = banks[0:2], banks[2:6], banks[6:8]

        pool_past, sp_past = sem("pool_past2"), sem("sp_past2")
        w_in = moe.w_in
        w_high = [sem(f"w{w}_high") for w in (1, 2)]
        w_done = [sem(f"w{w}_done") for w in (1, 2)]
        pick_ready, pick_hi, pick_done = sem("pick_ready"), sem("pick_hi"), sem("pick_done")
        up_ready, silu_done, hid_high, hid_done = sem("up_ready"), sem("silu_done"), sem("hid_high"), sem("hid_done")
        down_ready, mixed_done = sem("down_ready"), sem("mixed_done")
        added = [sem(f"added{g}") for g in range(EG)]

        def program(eng, steps_fn):
            same = lambda value, per_expert: value
            steps_fn(start_steps + expert_steps(0), same)
            with eng.Fori(1, E - 1) as e:
                steps_fn(expert_steps(1), lambda value, per_expert: e * per_expert + (value - per_expert))
            steps_fn(expert_steps(E - 1), same)

        block = mem.enter_context(nc.Block())

        @block.sync
        def _(sp):
            def steps(todo, at):
                for kind, n, k in todo:
                    sp.wait_ge(w_done[k], at(n, 1))
                    sp.sem_inc(sp_past, 1)
                    sp.dma_start(moe.w_raw[k], moe.w_view[k][at(n, 1)]).then_inc(w_in[k], 16)

            def ahead(todo, at):
                steps([(kind, n, k) for kind, n, k in todo if kind == "w" and n >= 1], at)

            program(sp, ahead)

        @block.gpsimd
        def _(pool):
            def steps(todo, at):
                for kind, n, k in todo:
                    grp = n % EG
                    if kind == "gather":
                        pool.wait_ge(sel_done, at(n + 1, EG))
                        if n >= 2:
                            pool.wait_ge(pick_ready, at(DT * (n - 1), EG * DT))
                        pool.sem_inc(pool_past, 1)
                        gather(nc, moe, xn_dram, n)
                    elif kind == "down" and k == GB4 // 2 - 1:
                        pool.wait_ge(mixed_done, at((GB4 // 2) * (n + 1), EG * GB4 // 2))
                        if n == 0:
                            pool.wait_ge(moe.out_stored, 16 * B)
                        if n >= EG:
                            pool.wait_ge(added[grp], at(16 * GB4 * (n // EG), 16 * GB4))
                        pool.sem_inc(pool_past, 1)
                        for j in range(GB4):
                            nc.gpsimd.indirect_dma_start(
                                out=out_rows, out_offset=bass.IndirectOffsetOnAxis(ap=row_sel[grp][:, j, :], axis=0),
                                in_=mixed[n % 2][:, j, :], in_offset=None, compute_op=ALU.add).then_inc(added[grp], 16)

            program(pool, steps)
            for g in range(EG):
                pool.wait_ge(added[g], 16 * GB4 * E)

        @block.scalar
        def _(act):
            def steps(todo, at):
                for kind, n, k in todo:
                    if kind == "w":
                        act.wait_ge(w_in[k], at(16 * (n + 1), 16))
                        if k == 0 and n >= 1:
                            act.wait_ge(up_ready, at(FT * EG * n, FT * EG))
                        elif n >= 1:
                            act.wait_ge(down_ready, at(GB4 // 2 * EG * n, GB4 // 2 * EG))
                        nc.scalar.activation(w_hi[k][:], moe.w_raw[k], ACT.Copy).then_inc(w_high[k], 1)
                    elif kind == "pick":
                        act.wait_ge(pick_ready, at(DT * n + k + 1, DT * EG))
                        nc.scalar.activation(pt_hi[:, k, :], PICK[k][:], ACT.Copy).then_inc(pick_hi, 1)
                    elif kind == "h":
                        act.wait_ge(up_ready, at(FT * n + k + 1, FT * EG))
                        if FT * n + k >= 2:
                            act.wait_ge(hid_done, at(FT * n + k - 1, FT * EG))
                        nc.scalar.activation(hid[k % 2][:], UP[k][:], ACT.Silu).then_inc(silu_done, 1)

            program(act, steps)

        @block.vector
        def _(dve):
            def steps(todo, at):
                for kind, n, k in todo:
                    grp = n % EG
                    if kind == "w":
                        dve.wait_ge(w_high[k], at(n + 1, 1))
                        nc.vector.tensor_tensor(w_lo[k][:], moe.w_raw[k], w_hi[k][:], ALU.subtract).then_inc(w_done[k], 1)
                    elif kind == "gather":
                        if n >= EG:
                            dve.wait_ge(added[grp], at(16 * GB4 * (n // EG), 16 * GB4))
                        select(nc, moe, n, at(n // EG, 1))
                    elif kind == "pick":
                        dve.wait_ge(pick_hi, at(DT * n + k + 1, DT * EG))
                        nc.vector.tensor_tensor(pt_lo[:, k, :], PICK[k][:], pt_hi[:, k, :], ALU.subtract).then_inc(pick_done, 1)
                    elif kind == "h":
                        u = FT * n + k
                        dve.wait_ge(silu_done, at(u + 1, FT * EG))
                        nc.vector.tensor_copy(hid_hi[n % 2][:, k, :], hid[k % 2][:]).then_inc(hid_high, 1)
                        dve.wait_ge(hid_high, at(u + 1, FT * EG))
                        nc.vector.tensor_tensor(hid_lo[n % 2][:, k, :], hid[k % 2][:], hid_hi[n % 2][:, k, :], ALU.subtract).then_inc(hid_done, 1)
                    elif kind == "down":
                        u = GB4 // 2 * n + k
                        dve.wait_ge(down_ready, at(u + 1, GB4 // 2 * EG))
                        dve.wait_ge(sel_done, at(n + 1, EG))
                        if n >= 2 and k == 0:
                            dve.wait_ge(added[(n - 2) % EG], at(16 * GB4 * ((n - 2) // EG + 1), 16 * GB4))
                        for t in range(2):
                            j = 2 * k + t
                            last = nc.vector.tensor_scalar(mixed[n % 2][:, j, :], DOWN[k][:, D * t:D * t + D],
                                                           gate_sel[grp][:, j, :], None, ALU.mult)
                        last.then_inc(mixed_done, 1)

            program(dve, steps)

        @block.tensor
        def _(pe):
            def steps(todo, at):
                for kind, n, k in todo:
                    if kind == "pick":
                        if k == 0:
                            pe.wait_ge(gathered[n % EG], at(16 * GB4 * (n // EG + 1), 16 * GB4))
                        if n >= 1:
                            pe.wait_ge(pick_done, at(DT * (n - 1) + k + 1, DT * EG))
                        for j in range(GB4):
                            last = nc.tensor.transpose(PICK[k][:, P * j:P * j + P], picked[n % 2][:, j, P * k:P * k + P], ident[:])
                        last.then_inc(pick_ready, 1)
                    elif kind == "h":
                        u = FT * n + k
                        if k == 0:
                            pe.wait_ge(pick_done, at(DT * (n + 1), DT * EG))
                            if n % EG == 0:
                                pe.wait_ge(w_done[0], at(n // EG + 1, 1))
                        if n >= 1:
                            pe.wait_ge(silu_done, at(u - FT + 1, FT * EG))
                        f = slice(P * k, P * k + P)
                        todo_mm = [(a[:, dt, f], b[:, dt, :]) for dt in range(DT)
                                   for a, b in ((w1_hi, pt_hi), (w1_hi, pt_lo), (w1_lo, pt_hi))]
                        for m, (a, b) in enumerate(todo_mm):
                            last = nc.tensor.matmul(UP[k][:], a, b, start=m == 0, stop=m == len(todo_mm) - 1)
                        last.then_inc(up_ready, 1)
                    elif kind == "down":
                        u = GB4 // 2 * n + k
                        if k == 0:
                            pe.wait_ge(hid_done, at(FT * (n + 1), FT * EG))
                            if n % EG == 0:
                                pe.wait_ge(w_done[1], at(n // EG + 1, 1))
                        if n >= 1:
                            pe.wait_ge(mixed_done, at(u - 1, GB4 // 2 * EG))
                        for t in range(2):
                            r = slice(P * (2 * k + t), P * (2 * k + t) + P)
                            todo_mm = [(a[:, ft, r], b[:, ft, :]) for ft in range(FT)
                                       for a, b in ((hid_hi[n % 2], w2_hi), (hid_hi[n % 2], w2_lo), (hid_lo[n % 2], w2_hi))]
                            for m, (a, b) in enumerate(todo_mm):
                                last = nc.tensor.matmul(DOWN[k][:, D * t:D * t + D], a, b, start=m == 0, stop=m == len(todo_mm) - 1)
                        last.then_inc(down_ready, 1)

            program(pe, steps)


_INS = ["L0_attn_hidden_states", "L0_attn_q_a", "L0_attn_q_b", "L0_attn_k_a", "L0_attn_k_b", "L0_attn_v_w",
        "L0_attn_v_b", "L0_attn_o_w", "L0_attn_o_b", "L0_ffn_choice_w", "L0_ffn_w1", "L0_ffn_w2"]


def kernel(**inputs):
    import numpy as np
    import concourse.bacc as bacc
    from concourse.bass_utils import run_bass_kernel_spmd

    nc = bacc.Bacc("TRN2", target_bir_lowering=False, num_devices=1)
    arrays, args = {}, []
    for name in _INS:
        a = np.ascontiguousarray(inputs[name])
        arrays[f"in_{name}"] = a
        args.append(nc.dram_tensor(f"in_{name}", a.shape, mybir.dt.from_np(a.dtype), kind="ExternalInput").ap())
    out = nc.dram_tensor("out_rows", (B, T, D), mybir.dt.float32, kind="ExternalOutput").ap()
    build(nc, *args, out)
    r = run_bass_kernel_spmd(nc, [arrays], core_ids=[0])
    return r.results[0]["out_rows"]
```

```python
import concourse.bass as bass
from concourse import mybir
from contextlib import ExitStack

B, T, D = 16, 512, 256
H, HD, R = 16, 16, 64
E, F = 8, 512
CAP = T * 2 // E
P = 128
TT, DT, FT = T // P, D // P, F // P
EPS = 1e-5
GH = 4
GB = H // GH
NG = B * GB
UN = 10
TERMS = ((0, 0), (0, 1), (1, 0), (0, 2), (2, 0), (1, 1))
KS = HD * len(TERMS)
SHIFT = 2
NEG = -1e30
GB4 = 4
EG = B // GB4
SCALE = 1.0 / HD ** 0.5


def unit_parts(t, transposed):
    pair, r = divmod(t, 5)
    a, b = 2 * pair, 2 * pair + 1
    parts = [[(a, 3)], [(a, 2), (a, 0)], [(a, 1), (b, 1)], [(b, 3)], [(b, 2), (b, 0)]][r]
    out, col = [], 0
    for h, i in parts:
        out.append((h, 3 - i if transposed else i, col, P * (i + 1)))
        col += P * (i + 1)
    return out


PROJECTIONS = (
    [(0, "v", 1, 0), (1, "mid", 1, 3), (1, "yt", -1, 0), (2, "xload", 2, 0), (6, "yt", -1, 1), (8, "v", 1, 1),
     (9, "lnstat", 2, 0), (9, "v", 1, 2)],
    [(0, "v", 1, 3), (1, "lnstat", 2, 1), (2, "o", -1, 0), (5, "lnapply", 2, 0), (5, "o", -1, 1), (6, "o", -1, 2),
     (8, "o", -1, 3)],
    [(0, "xt", 2, 0), (1, "xres", 0, 0), (1, "xt", 2, 1), (6, "qk_first", 2, 0), (8, "qk", 2, 0),
     (9, "qk_first", 2, 1)],
    [(0, "qk", 2, 1), (0, "mid", 2, 0), (1, "mid", 2, 1), (4, "qk_first", 2, 2), (6, "qk", 2, 2), (8, "mid", 2, 2),
     (8, "qk_first", 2, 3), (9, "qk", 2, 3)])
SUMS = (
    [(2, "pv", 0, 0), (3, "pv", 0, 1), (4, "pv", 0, 2), (4, "maxt", 2, 0), (5, "pv", 0, 3), (7, "ytr", 0, 0)],
    [(2, "pv", 0, 0), (3, "pv", 0, 1), (4, "pv", 0, 2), (4, "maxt", 2, 0), (6, "pv", 0, 3), (7, "ytr", 0, 0)],
    [(2, "pv", 0, 0), (3, "pv", 0, 1), (4, "pv", 0, 2), (4, "maxt", 2, 0), (5, "pv", 0, 3), (7, "ytr", 0, 0)],
    [(2, "pv", 0, 0), (3, "pv", 0, 1), (4, "pv", 0, 2), (4, "maxt", 2, 0), (5, "pv", 0, 3), (7, "ytr", 0, 0)])


def slot_steps(b, g):
    G = GB * b + g
    put = {t: [] for t in range(UN)}
    for t, kind, ahead, k in SUMS[g]:
        if G + ahead < NG:
            put[t].append((kind, G + ahead, k))
    last_values = b == B - 2
    if last_values and g == 0:
        put[0].append(("v", b + 1, 0))
        put[1].append(("v", b + 1, 1))
        put[3].append(("v", b + 1, 2))
        put[4].append(("v", b + 1, 3))
    for t, kind, ahead, k in PROJECTIONS[g]:
        if last_values and kind == "v":
            continue
        if 0 <= b + ahead < B and (kind, b + ahead) != ("mid", 1):
            put[t].append((kind, b + ahead, k))
    for t, step in routing_steps(G):
        put[t].append(step)
    out = []
    for t in range(UN):
        out += [("scoret", G + 1, t)] * (G + 1 < NG) + [("score", G + 3, t)] * (G + 3 < NG) + put[t]
    return out


RANK_OPS = 3 * (CAP // 8) - 1
RANK_PLACES = {7: (4, 5, 6, 8, 9), 6: (0, 1, 3, 4, 6, 7), 5: (0, 1, 3, 4, 6, 7), 4: (0, 1, 3, 4, 6, 7),
               3: range(8), 2: range(8), 1: range(8)}


def routing_steps(G):
    left = NG - G
    if left == 8:
        return [(5, ("gate_max", 0, 0)), (6, ("gate_max", 0, 1)), (7, ("gate_exp", 0, 0)), (8, ("gate_norm", 0, 0)),
                (9, ("gate_norm", 0, 1))]
    out = [(0, ("gate_norm", 0, 2)), (2, ("rankt", 0, 0)), (3, ("first_row", 0, 0))] if left == 7 else []
    per_slot = RANK_PLACES
    done = sum(len(places) for later, places in per_slot.items() if later > left)
    if left in per_slot:
        out += [(t, ("rank", done + m, 0)) for m, t in enumerate(per_slot[left])]
        assert sum(map(len, per_slot.values())) == RANK_OPS
    if left == 5:
        out += [(0, ("w_load", 0, 0))]
    if left == 1:
        out += [(9, ("rows", 0, 0))]
    return out


def prologue_steps():
    foldt = lambda n: [("foldt", n, half) for half in range(2)]
    qk = lambda b, mt: [("qk_first", b, mt), ("qk", b, mt)]
    out = [("xload", 0, 0), ("lnstat", 0, 0), ("lnstat", 0, 1), ("lnapply", 0, 0), ("xload", 1, 0)]
    out += foldt(0) + [("fold", 0, 0)] + foldt(1) + [("xt", 0, 0), ("xt", 0, 1), ("fold", 1, 0)]
    out += foldt(2) + qk(0, 0) + foldt(3) + qk(0, 1)
    out += [("mid", 0, 0), ("fold", 2, 0), ("mid", 0, 1), ("fold", 3, 0), ("wv", 0, 0), ("wv", 1, 0)]
    out += [("lnstat", 1, 0), ("lnstat", 1, 1)] + qk(0, 2) + qk(0, 3)
    out += [("mid", 0, 2), ("v", 0, 0), ("mid", 0, 3), ("v", 0, 1), ("v", 0, 2), ("lnapply", 1, 0), ("v", 0, 3)]
    out += [("xt", 1, dt) for dt in range(DT)] + [("wo", dt, 0) for dt in range(DT)]
    for t in range(UN):
        out.append(("score", 0, t))
        if t in (0, 2, 4, 6):
            out += qk(1, t // 2)
        if t in (2, 4, 6):
            out.append(("mid", 1, t // 2 - 1))
    for t in range(UN):
        out += [("score", 1, t)] + [("maxt", 0, 0)] * (t == 2) + [("mid", 1, 3)] * (t == 4)
    for t in range(UN):
        out += [("scoret", 0, t), ("score", 2, t)] + [("maxt", 1, 0)] * (t == 3)
    return out


def epilogue_steps():
    return [("yt", B - 1, 0), ("rowst", 0, 0), ("gather", 0, 0), ("yt", B - 1, 1)] \
        + [("o", B - 1, tt) for tt in range(TT)]


def pair_steps(i):
    return [s for b in (2 * i, 2 * i + 1) for g in range(GB) for s in slot_steps(b, g)]


class Handover:

    def __init__(self, rows, gates, row_sel, gate_sel, w_raw, picked, w_in, w_view, sel_done, gathered, out_stored):
        self.rows = rows
        self.gates = gates
        self.row_sel = row_sel
        self.gate_sel = gate_sel
        self.w_raw = w_raw
        self.picked = picked
        self.w_in = w_in
        self.w_view = w_view
        self.sel_done = sel_done
        self.gathered = gathered
        self.out_stored = out_stored


def build(nc, x, q_a, q_b, k_a, k_b, v_w, v_b, o_w, o_b, choice_w, w1, w2, out):
    fp32, f32r, bf16 = mybir.dt.float32, mybir.dt.float32r, mybir.dt.bfloat16
    i32, u32 = mybir.dt.int32, mybir.dt.uint32
    ALU, ACT, AX = mybir.AluOpType, mybir.ActivationFunctionType, mybir.AxisListType

    PAIRS = B // 2
    every = prologue_steps() + [s for i in range(PAIRS) for s in pair_steps(i)] + epilogue_steps()
    shared = [s for s in every if s[0] in ("foldt", "fold", "wv", "wo", "xt", "qk", "v", "maxt", "ytr", "yt", "o",
                                            "rankt", "rowst")]
    unit_of = {s: n for n, s in enumerate(shared)}
    split_of = {s: n for n, s in enumerate(s for s in shared if s[0] in ("fold", "wv", "wo", "xt", "qk", "yt"))}
    U_PAIR, S_PAIR = 48, 16
    for i in range(1, PAIRS - 2):
        for s, z in zip(pair_steps(i), pair_steps(i + 1)):
            assert s not in unit_of or unit_of[z] - unit_of[s] == U_PAIR
            assert s not in split_of or split_of[z] - split_of[s] == S_PAIR

    x_v = x.rearrange("b (t p) d -> b p t d", p=P)
    out_v = out.rearrange("b (t p) d -> b p t d", p=P)
    out_rows = out.rearrange("b t d -> (b t) d")
    xn_dram = nc.dram_tensor("xn_rows", (B * T, D), fp32, kind="Internal").ap()
    xn_v = xn_dram.rearrange("(b t p) d -> b p t d", b=B, p=P)

    ctx = ExitStack()
    with ctx:
        def sem(name):
            return ctx.enter_context(nc.semaphore(name))

        def keep(name, shape, dt):
            return ctx.enter_context(nc.sbuf_tensor(name, shape, dt))

        ident = keep("ident", [P, P], fp32)
        ident_bf = keep("ident_bf", [P, P], bf16)
        logits = keep("logits", [P, TT, B, E], fp32)
        qstk, kstk = [keep("qstk0", [P, H, T], bf16)], [keep("kstk0", [P, H, T], bf16)]
        xres = keep("xres", [P, TT, D], fp32)
        stack32 = [t[0][:].rearrange("p h t -> p (h t)").bitcast(fp32) for t in (qstk, kstk)]
        quarter = lambda which, n: stack32[which][:, 1024 * n:1024 * n + 1024]
        rows = keep("rows", [P, B, E], u32)
        gates = keep("gates", [P, B, E], fp32)
        moe = Handover(
            rows=rows, gates=gates,
            row_sel=[keep(f"row_sel{g}", [P, GB4, 1], u32) for g in range(EG)],
            gate_sel=[keep(f"gate_sel{g}", [P, GB4, 1], fp32) for g in range(EG)],
            w_raw=[quarter(w, 0) for w in range(2)],
            picked=[quarter(w, 1).rearrange("p (j d) -> p j d", j=GB4) for w in range(2)],
            w_in=[sem(f"w{w}_in") for w in (1, 2)],
            w_view=[w1.rearrange("e (t p) f -> e p t f", p=P), w2.rearrange("e (t p) d -> e p t d", p=P)],
            sel_done=sem("sel_done"),
            gathered=[sem(f"gathered{g}") for g in range(EG)],
            out_stored=sem("out_stored"))
        banks = [ctx.enter_context(nc.psum_tensor(f"bank{i}", [P, 512], fp32)) for i in range(8)]

        with ExitStack() as mem:
            def sb(name, shape, dt):
                return mem.enter_context(nc.sbuf_tensor(name, shape, dt))

            qstk.append(sb("qstk1", [P, H, T], bf16))
            kstk.append(sb("kstk1", [P, H, T], bf16))
            vaug = [sb(f"vaug{u}", [P, TT, H, 2 * HD], fp32) for u in range(2)]
            probs = [sb(f"probs{u}", [P, 2 * 5 * 512], fp32) for u in range(2)]
            xln = sb("xln", [P, TT, D], fp32)
            xn = sb("xn", [P, TT, D], fp32)
            xt_hi = sb("xt_hi", [P, DT, T], f32r)
            xt_lo = sb("xt_lo", [P, DT, T], f32r)
            rest = [sb(f"rest{u}", [P, T], fp32) for u in range(2)]
            qk_part = [sb(f"qk_part{n}", [P, 4, T], bf16) for n in range(3)]
            yraw = [sb(f"yraw{u}", [P, T], fp32) for u in range(2)]
            ytok = sb("ytok", [P, TT, D], fp32)
            yt_hi = sb("yt_hi", [P, DT, T], f32r)
            yt_lo = sb("yt_lo", [P, DT, T], f32r)
            junk = [sb(f"junk{u}", [P, 512], bf16) for u in range(2)]
            maxrow = [sb(f"maxrow{u}", [SHIFT * GH * TT, P], bf16) for u in range(2)]
            rowmax = [sb(f"rowmax{u}", [P, GH, TT], fp32) for u in range(2)]
            negmax = [sb(f"negmax{u}", [P, SHIFT, GH, TT], bf16) for u in range(2)]
            rden = sb("rden", [P, TT, GH], fp32)
            stats = sb("stats", [P, TT, 6], fp32)
            meanvar = sb("meanvar", [P, TT, 2], fp32)
            vareps = sb("vareps", [P, TT], fp32)
            rstd = sb("rstd", [P, TT], fp32)
            ones_bf = sb("ones_bf", [P, H * T * SHIFT // P], bf16)
            mhalf = sb("mhalf", [P, TT], fp32)
            eps = sb("eps", [P, TT], fp32)
            wqk_hi = sb("wqk_hi", [P, DT, 2 * D], f32r)
            wqk_lo = sb("wqk_lo", [P, DT, 2 * D], f32r)
            wv_hi = sb("wv_hi", [P, DT, D + E], f32r)
            wv_lo = sb("wv_lo", [P, DT, D + E], f32r)
            wo_hi = sb("wo_hi", [P, DT, D], f32r)
            wo_lo = sb("wo_lo", [P, DT, D], f32r)
            vb_all = sb("vb_all", [P, D], fp32)
            ob_all = sb("ob_all", [P, D], fp32)
            rowmask = sb("rowmask", [P, T], fp32)
            colmask = sb("colmask", [P, P], bf16)
            fold_raw = [probs[w][:, 0:DT * H * R].rearrange("p (t h r) -> p t h r", t=DT, h=H) for w in range(2)]
            vw_raw = probs[0][:, 2048:2560].rearrange("p (t d) -> p t d", t=DT)
            ow_raw = probs[1][:, 2048:2560].rearrange("p (t d) -> p t d", t=DT)
            choice_raw = probs[0][0:E, 2560:2560 + D]
            foldb = probs[1][:, 2560:2560 + 2 * D].rearrange("p (w c j) -> p w c j", w=2, c=H // 2)
            fold_t = [[probs[half][:, 3072 + 512 * n:3584 + 512 * n] for half in range(2)] for n in range(2 * DT)]

            dve_past, sp_past = sem("dve_past"), sem("sp_past")
            fold_a_in = [sem(f"fold_a_in{n}") for n in range(2 * DT)]
            fold_b_in = [sem(f"fold_b_in{w}") for w in range(2)]
            weights_in = sem("weights_in")
            out_weights_in = sem("out_weights_in")
            ident_done = sem("ident_done")
            ones_done = sem("ones_done")
            ones_in = sem("ones_in")
            consts = sem("consts")
            zeroed = sem("zeroed")
            foldb_zero = sem("foldb_zero")
            x_in = sem("x_in")
            stats_done = sem("stats_done")
            mv_done = sem("mv_done")
            vareps_done = sem("vareps_done")
            rstd_done = sem("rstd_done")
            xn_done = sem("xn_done")
            xn_stored = sem("xn_stored")
            shared_ready = [sem(f"shared_ready{u}") for u in range(2)]
            shared_done = [sem(f"shared_done{u}") for u in range(2)]
            hi_done = sem("hi_done")
            mid_done = sem("mid_done")
            lo_done = sem("lo_done")
            stacked = [sem(f"stacked{u}") for u in range(2)]
            logit_done = sem("logit_done")
            score_ready = sem("score_ready")
            score_done = sem("score_done")
            neghi_done = sem("neghi_done")
            negmax_done = sem("negmax_done")
            max_in = [sem(f"max_in{u}") for u in range(2)]
            scoret_ready = sem("scoret_ready")
            exp_done = sem("exp_done")
            pv_ready = sem("pv_ready")
            yraw_done = sem("yraw_done")
            rden_done = sem("rden_done")
            xres_in = sem("xres_in")
            xres_done = sem("xres_done")
            out_stored = moe.out_stored
            gate_step = sem("gate_step")
            gate_exp = sem("gate_exp")
            first_step = sem("first_step")
            ids = sem("ids")

            xn_flat, xln_flat = (t[:].rearrange("p t d -> p (t d)") for t in (xn, xln))
            gate = xn_flat[:, 0:T].rearrange("p (t r) -> p t r", t=TT)
            top, top_row = xn_flat[:, T:T + CAP], xn_flat[:, T + CAP:T + 2 * CAP]
            top_at = xn_flat[:, T + 2 * CAP:T + 3 * CAP].bitcast(u32)
            gsum = xn_flat[:, T + 3 * CAP:T + 3 * CAP + TT * B]
            ranked = [xln_flat[:, T * u:T * u + T] for u in range(2)]
            first_i = [sb(f"first_i{u}", [P, 1], i32) for u in range(3)]
            first = sb("first", [P, 1], fp32)
            GATED = 5

            SCORE, SCORET, Y, SHARED = banks[0:3], banks[3:5], banks[5], banks[6:8]
            FIRST, PER_PAIR = UN * 3, UN * GB * 2

            def score_bank(u):
                return (u if u < FIRST else (u - FIRST) % PER_PAIR) % 3

            def score_back(u):
                return next(d for d in range(1, 6) if score_bank(u - d) == score_bank(u))

            N_CONST = 5
            STACK_DMAS = 16 * 2 * len(TERMS)
            N_WEIGHTS, N_OUT_WEIGHTS = 16 * 3, 16 * 2

            def program(eng, steps_fn):
                same = lambda value, per_pair: value
                steps_fn(prologue_steps() + pair_steps(0), same)
                with eng.Fori(1, PAIRS - 1) as i:
                    steps_fn(pair_steps(1), lambda value, per_pair: i * per_pair + (value - per_pair))
                steps_fn(pair_steps(PAIRS - 1) + epilogue_steps(), same)

            def bank_of(step):
                return unit_of[step] % 2

            def filled(step, at):
                return at(unit_of[step] // 2 + 1, U_PAIR // 2)

            def emptied(step, at):
                return at(unit_of[step] // 2 + 1, U_PAIR // 2)

            def split(step, at):
                return at(split_of[step] + 1, S_PAIR)

            block = mem.enter_context(nc.Block())

            @block.sync
            def _(sp):
                def first_factors(w, raw):
                    for dt in range(DT):
                        sp.dma_start(fold_raw[w][:, dt, :, :], raw[:, P * dt:P * dt + P, :].rearrange("h p r -> p h r"))\
                            .then_inc(fold_a_in[DT * w + dt], 16)

                def ones():
                    sp.wait_ge(ones_done, 1)
                    for u in range(2):
                        sp.dma_start(kstk[u][KS:KS + SHIFT, :, :], ones_bf[:]).then_inc(ones_in, 16)

                def steps(todo, at):
                    for step in todo:
                        kind, n, k = step
                        if kind == "xload":
                            if n >= 1:
                                sp.wait_ge(xn_done, at(n, 2))
                                sp.sem_inc(sp_past, 1)
                            sp.dma_start(xln[:], x_v[at(n, 2)]).then_inc(x_in, 16)
                            if n == 0:
                                first_factors(0, q_a)
                                ones()
                                first_factors(1, k_a)
                        elif kind == "lnapply":
                            sp.wait_ge(xn_done, at(n + 1, 2))
                            sp.sem_inc(sp_past, 1)
                            sp.dma_start(xn_v[at(n, 2)], xn[:]).then_inc(xn_stored, 16)
                        elif kind == "mid" and k % 2 == 1:
                            if n >= 2 and k == 1:
                                sp.wait_ge(scoret_ready, at(UN * GB * (n - 1), 8 * UN))
                                sp.sem_inc(sp_past, 1)
                            sp.wait_ge(lo_done, at(GB * n + k + 1, 2 * GB))
                            side = k // 2
                            stk = (qstk, kstk)[side][n % 2]
                            for t, term in enumerate(TERMS):
                                sp.dma_start(stk[HD * t:HD * t + HD, :, :],
                                             qk_part[term[side]][:, 2 * side:2 * side + 2, :]).then_inc(stacked[n % 2], 16)
                        elif kind == "maxt":
                            sp.wait_ge(shared_done[bank_of(step)], emptied(step, at))
                            sp.sem_inc(sp_past, 1)
                            b, g = divmod(n, GB)
                            for s in range(SHIFT):
                                sp.dma_start(qstk[b % 2][KS + s:KS + s + 1, GH * g:GH * g + GH, :],
                                             maxrow[n % 2][GH * TT * s:GH * TT * (s + 1), :]).then_inc(max_in[n % 2], 16)
                        elif kind == "xres":
                            if n >= 1:
                                sp.wait_ge(out_stored, at(16 * n, 32))
                                sp.sem_inc(sp_past, 1)
                            sp.dma_start(xres[:], x_v[at(n, 2)]).then_inc(xres_in, 16)
                        elif kind == "o" and k == TT - 1:
                            sp.wait_ge(shared_done[bank_of(step)], emptied(step, at))
                            sp.sem_inc(sp_past, 1)
                            sp.wait_ge(shared_done[bank_of(("o", n, TT - 2))], emptied(("o", n, TT - 2), at))
                            sp.sem_inc(sp_past, 1)
                            sp.dma_start(out_v[at(n, 2)], xres[:]).then_inc(out_stored, 16)

                        elif kind == "w_load":
                            sp.wait_ge(scoret_ready, UN * GB * (B - 1))
                            for w in range(2):
                                sp.dma_start(moe.w_raw[w], moe.w_view[w][0]).then_inc(moe.w_in[w], 16)

                program(sp, steps)

            @block.gpsimd
            def _(pool):
                nc.gpsimd.memset(ident[:], 0.0).then_inc(zeroed, 1)
                nc.gpsimd.memset(mhalf[:], -0.5).then_inc(consts, 1)
                nc.gpsimd.memset(eps[:], EPS).then_inc(consts, 1)
                pool.wait_ge(zeroed, 1)
                nc.gpsimd.affine_select(out=ident[:], in_=ident[:], compare_op=ALU.not_equal, fill=1.0, base=0,
                                        pattern=[[-1, P]], channel_multiplier=1).then_inc(ident_done, 1)
                nc.gpsimd.memset(ident_bf[:], 0.0).then_inc(zeroed, 1)
                nc.gpsimd.memset(colmask[:], 0.0).then_inc(zeroed, 1)
                nc.gpsimd.memset(rowmask[:], 0.0).then_inc(zeroed, 1)
                pool.wait_ge(zeroed, 4)
                nc.gpsimd.affine_select(out=ident_bf[:], in_=ident_bf[:], compare_op=ALU.not_equal, fill=1.0, base=0,
                                        pattern=[[-1, P]], channel_multiplier=1).then_inc(consts, 1)
                nc.gpsimd.affine_select(out=colmask[:], in_=colmask[:], compare_op=ALU.is_ge, fill=NEG, base=0,
                                        pattern=[[-1, P]], channel_multiplier=1).then_inc(consts, 1)
                nc.gpsimd.affine_select(out=rowmask[:, T - P:T], in_=rowmask[:, T - P:T], compare_op=ALU.is_ge,
                                        fill=NEG, base=0, pattern=[[-1, P]], channel_multiplier=1).then_inc(consts, 1)
                nc.gpsimd.iota(first_i[0][:], pattern=[[0, 1]], base=0, channel_multiplier=1).then_inc(ids, 1)

                def steps(todo, at):
                    for step in todo:
                        kind, n, k = step
                        if kind == "gather":
                            pool.wait_ge(moe.sel_done, n + 1)
                            pool.wait_ge(xn_stored, 16 * B)
                            gather(nc, moe, xn_dram, n)
                        elif kind == "lnstat" and k == 1:
                            pool.wait_ge(mv_done, at(n + 1, 2))
                            if n >= 1:
                                pool.wait_ge(xn_done, at(n, 2))
                            nc.gpsimd.tensor_tensor(vareps[:], meanvar[:, :, 1], eps[:], ALU.add).then_inc(vareps_done, 1)
                            pool.wait_ge(vareps_done, at(n + 1, 2))
                            nc.gpsimd.tensor_tensor(rstd[:], vareps[:], mhalf[:], ALU.pow).then_inc(rstd_done, 1)
                        elif kind == "mid":
                            pool.wait_ge(mid_done, at(GB * n + k + 1, 2 * GB))
                            if n >= 1:
                                pool.wait_ge(stacked[(n - 1) % 2], at(STACK_DMAS * ((n - 1) // 2 + 1), STACK_DMAS))
                            nc.gpsimd.tensor_tensor(qk_part[2][:, k, :], rest[k % 2][:], qk_part[1][:, k, :],
                                                    ALU.subtract).then_inc(lo_done, 1)
                        elif kind == "xres":
                            pool.wait_ge(xres_in, at(16 * (n + 1), 32))
                            if n == 0:
                                pool.wait_ge(out_weights_in, N_OUT_WEIGHTS)
                            nc.gpsimd.tensor_tensor(xres[:], xres[:], ob_all[:].unsqueeze(1).to_broadcast([P, TT, D]),
                                                    ALU.add).then_inc(xres_done, 1)

                program(pool, steps)

            @block.scalar
            def _(act):
                act.wait_ge(foldb_zero, 1)
                def second_factors(w, raw):
                    for odd in range(2):
                        act.dma_start(foldb[R * odd:R * odd + R, w, :, HD * odd:HD * odd + HD],
                                      raw.rearrange("(c two) r j -> two r c j", two=2)[odd]).then_inc(fold_b_in[w], 16)

                second_factors(0, q_b)
                second_factors(1, k_b)
                act.dma_start(vw_raw, v_w.rearrange("(t p) d -> p t d", p=P)).then_inc(weights_in, 16)
                act.dma_start(choice_raw, choice_w).then_inc(weights_in, 16)
                act.dma_start(vb_all[:], v_b.partition_broadcast(P)).then_inc(weights_in, 16)
                act.dma_start(ow_raw, o_w.rearrange("(t p) d -> p t d", p=P)).then_inc(out_weights_in, 16)
                act.dma_start(ob_all[:], o_b.partition_broadcast(P)).then_inc(out_weights_in, 16)

                def steps(todo, at):
                    for step in todo:
                        kind, n, k = step
                        if step in unit_of:
                            p, src = bank_of(step), SHARED[bank_of(step)]
                        if kind == "gate_exp":
                            act.wait_ge(gate_step, 2)
                            nc.scalar.activation(gate, gate, ACT.Exp).then_inc(gate_exp, 1)
                        elif kind == "rankt":
                            act.wait_ge(shared_ready[p], filled(step, at))
                            act.wait_ge(xn_done, B)
                            nc.scalar.activation(ranked[0], src[:], ACT.Copy).then_inc(shared_done[p], 1)
                        elif kind == "foldt" and k == 0:
                            act.wait_ge(shared_ready[p], filled(step, at))
                            nc.scalar.activation(fold_t[n][0], src[:], ACT.Copy).then_inc(shared_done[p], 1)
                        elif kind == "fold":
                            act.wait_ge(shared_ready[p], filled(step, at))
                            w, dt = divmod(n, DT)
                            nc.scalar.activation(
                                wqk_hi[:, dt, D * w:D * w + D].rearrange("p (m j h) -> p m h j", m=2, h=8),
                                src[:, 0:D].rearrange("p (h m j) -> p m h j", m=2, h=8), ACT.Copy).then_inc(hi_done, 1)
                        elif kind == "wv":
                            act.wait_ge(shared_ready[p], filled(step, at))
                            nc.scalar.activation(wv_hi[:, n, :], src[:, 0:D + E], ACT.Copy).then_inc(hi_done, 1)
                        elif kind == "wo":
                            act.wait_ge(shared_ready[p], filled(step, at))
                            nc.scalar.activation(wo_hi[:, n, :], src[:, 0:D], ACT.Copy).then_inc(hi_done, 1)
                        elif kind == "xt":
                            act.wait_ge(shared_ready[p], filled(step, at))
                            nc.scalar.activation(xt_hi[:, k, :], src[:], ACT.Copy).then_inc(hi_done, 1)
                        elif kind == "yt":
                            act.wait_ge(shared_ready[p], filled(step, at))
                            nc.scalar.activation(yt_hi[:, k, :], src[:], ACT.Copy).then_inc(hi_done, 1)
                        elif kind == "qk":
                            act.wait_ge(shared_ready[p], filled(step, at))
                            if n >= 1 and k == 0:
                                act.wait_ge(stacked[(n - 1) % 2], at(STACK_DMAS * ((n - 1) // 2 + 1), STACK_DMAS))
                            nc.scalar.activation(qk_part[0][:, k, :], src[:], ACT.Copy).then_inc(hi_done, 1)
                        elif kind == "mid":
                            qk = ("qk", n, k)
                            act.wait_ge(shared_done[bank_of(qk)], emptied(qk, at))
                            nc.scalar.activation(qk_part[1][:, k, :], rest[k % 2][:], ACT.Copy).then_inc(mid_done, 1)
                        elif kind == "v":
                            act.wait_ge(shared_ready[p], filled(step, at))
                            nc.scalar.activation(logits[:, k, at(n, 2), :], src[:, D:D + E], ACT.Copy).then_inc(logit_done, 1)
                        elif kind == "maxt":
                            act.wait_ge(shared_ready[p], filled(step, at))
                            if n >= 2:
                                act.wait_ge(max_in[n % 2], at(32 * (n // 2), 128))
                            nc.scalar.activation(maxrow[n % 2][:], src[:].bitcast(bf16)[0:SHIFT * GH * TT, 0:P], ACT.Copy)\
                                .then_inc(shared_done[p], 1)
                        elif kind == "scoret":
                            act.wait_ge(scoret_ready, at(UN * n + k + 1, 8 * UN))
                            if k == 0 and n >= 2:
                                act.wait_ge(pv_ready, at(n - 1, 8))
                            nc.scalar.activation(probs[n % 2][:, 512 * k:512 * k + 512], SCORET[k % 2][:], ACT.Exp,
                                                 scale=SCALE).then_inc(exp_done, 1)
                        elif kind == "pv" and k == TT - 1:
                            act.wait_ge(pv_ready, at(n + 1, 8))
                            nc.scalar.activation(yraw[n % 2][:], Y[:], ACT.Copy).then_inc(yraw_done, 1)

                program(act, steps)

            @block.vector
            def _(dve):
                nc.vector.memset(foldb, 0.0).then_inc(foldb_zero, 1)
                nc.vector.memset(ones_bf[:], 1.0).then_inc(ones_done, 1)
                for u in range(2):
                    nc.vector.memset(vaug[u][:, :, :, HD:2 * HD], 1.0).then_inc(ones_done, 1)
                log_v = logits[:].rearrange("p t b e -> p (t b) e")
                gate_e = gate.rearrange("p t (b e) -> p (t b) e", e=E)
                over_e = gsum.unsqueeze(2).to_broadcast([P, TT * B, E])
                by_be = lambda t: t[:].rearrange("p b e -> p (b e)")

                def take_low(step, at, low, whole, high):
                    p = bank_of(step)
                    dve.wait_ge(hi_done, split(step, at))
                    nc.vector.tensor_tensor(low, whole, high, ALU.subtract).then_inc(shared_done[p], 1)

                def steps(todo, at):
                    for step in todo:
                        kind, n, k = step
                        if step in unit_of:
                            p, src = bank_of(step), SHARED[bank_of(step)]
                        if kind == "gate_max" and k == 0:
                            dve.wait_ge(logit_done, B * TT)
                            dve.wait_ge(xn_stored, 16 * B)
                            prev = ("xt", B - 1, 1)
                            dve.wait_ge(shared_ready[bank_of(prev)], filled(prev, at))
                            nc.vector.reduce_max(gsum, log_v, AX.X).then_inc(gate_step, 1)
                        elif kind == "gate_max":
                            dve.wait_ge(gate_step, 1)
                            nc.vector.tensor_tensor(gate_e, log_v, over_e, ALU.subtract).then_inc(gate_step, 1)
                        elif kind == "gate_norm" and k == 0:
                            dve.wait_ge(gate_exp, 1)
                            nc.vector.reduce_sum(gsum, gate_e, AX.X).then_inc(gate_step, 1)
                        elif kind == "gate_norm" and k == 1:
                            dve.wait_ge(gate_step, 3)
                            nc.vector.reciprocal(gsum, gsum).then_inc(gate_step, 1)
                        elif kind == "gate_norm":
                            dve.wait_ge(gate_step, 4)
                            nc.vector.tensor_tensor(gate_e, gate_e, over_e, ALU.mult).then_inc(gate_step, 1)
                        elif kind == "first_row":
                            dve.wait_ge(ids, 1)
                            nc.vector.tensor_single_scalar(first_i[1][:], first_i[0][:], E.bit_length() - 1,
                                                           ALU.arith_shift_right).then_inc(first_step, 1)
                            dve.wait_ge(first_step, 1)
                            nc.vector.tensor_single_scalar(first_i[2][:], first_i[1][:], T.bit_length() - 1,
                                                           ALU.logical_shift_left).then_inc(first_step, 1)
                            dve.wait_ge(first_step, 2)
                            nc.vector.tensor_copy(first[:], first_i[2][:]).then_inc(first_step, 1)
                        elif kind == "rank":
                            if n == 0:
                                prev = ("rankt", 0, 0)
                                dve.wait_ge(shared_done[bank_of(prev)], emptied(prev, at))
                            dve.wait_ge(gate_step, GATED + n)
                            r, op = divmod(n, 3)
                            a, z, eight = ranked[r % 2], ranked[(r + 1) % 2], slice(8 * r, 8 * r + 8)
                            if op == 0:
                                last = nc.vector.max(top[:, eight], a)
                            elif op == 1:
                                last = nc.vector.max_index(top_at[:, eight], top[:, eight], a)
                            else:
                                last = nc.vector.match_replace(z, top[:, eight], a, -1.0)
                            last.then_inc(gate_step, 1)
                        elif kind == "rows":
                            dve.wait_ge(gate_step, GATED + RANK_OPS)
                            nc.vector.tensor_copy(top_row, top_at).then_inc(gate_step, 1)
                            dve.wait_ge(gate_step, GATED + RANK_OPS + 1)
                            dve.wait_ge(first_step, 3)
                            nc.vector.tensor_scalar(top_row, top_row, first[:], None, ALU.add).then_inc(gate_step, 1)
                        elif kind == "rowst":
                            dve.wait_ge(shared_ready[p], filled(step, at))
                            nc.vector.tensor_copy(by_be(rows), src[:, 0:P]).then_inc(gate_step, 1)
                            nc.vector.tensor_copy(by_be(gates), src[:, P:2 * P]).then_inc(shared_done[p], 1)
                        elif kind == "gather":
                            if n == 0:
                                prev = ("rowst", 0, 0)
                                dve.wait_ge(gate_step, GATED + RANK_OPS + 3)
                                dve.wait_ge(shared_done[bank_of(prev)], emptied(prev, at))
                            select(nc, moe, n, 0)
                        elif kind == "lnstat":
                            dve.wait_ge(x_in, at(16 * (n + 1), 32))
                            for tt in (2 * k, 2 * k + 1):
                                last = nc.vector.bn_stats(stats[:, tt, :], xln[:, tt, :])
                            last.then_inc(stats_done, 1)
                            if k == 1:
                                dve.wait_ge(stats_done, at(2 * (n + 1), 4))
                                dve.sem_inc(dve_past, 1)
                                for tt in range(TT):
                                    last = nc.vector.bn_aggr(meanvar[:, tt, :], stats[:, tt, :])
                                last.then_inc(mv_done, 1)
                        elif kind == "lnapply":
                            dve.wait_ge(rstd_done, at(n + 1, 2))
                            if n >= 1:
                                dve.wait_ge(xn_stored, at(16 * n, 32))
                                prev = ("xt", n - 1, 1)
                                dve.wait_ge(shared_ready[bank_of(prev)], filled(prev, at))
                            for tt in range(TT):
                                last = nc.vector.tensor_scalar(xn[:, tt, :], xln[:, tt, :], meanvar[:, tt, 0:1],
                                                               rstd[:, tt:tt + 1], ALU.subtract, ALU.mult)
                            last.then_inc(xn_done, 1)
                        elif kind == "foldt" and k == 1:
                            dve.wait_ge(shared_ready[p], filled(step, at))
                            nc.vector.tensor_copy(fold_t[n][1], src[:]).then_inc(shared_done[p], 1)
                        elif kind == "fold":
                            w, dt = divmod(n, DT)
                            view = "p (m j h) -> p m h j"
                            take_low(step, at, wqk_lo[:, dt, D * w:D * w + D].rearrange(view, m=2, h=8),
                                     src[:, 0:D].rearrange("p (h m j) -> p m h j", m=2, h=8),
                                     wqk_hi[:, dt, D * w:D * w + D].rearrange(view, m=2, h=8))
                        elif kind == "wv":
                            take_low(step, at, wv_lo[:, n, :], src[:, 0:D + E], wv_hi[:, n, :])
                        elif kind == "wo":
                            take_low(step, at, wo_lo[:, n, :], src[:, 0:D], wo_hi[:, n, :])
                        elif kind == "xt":
                            take_low(step, at, xt_lo[:, k, :], src[:], xt_hi[:, k, :])
                        elif kind == "yt":
                            take_low(step, at, yt_lo[:, k, :], src[:], yt_hi[:, k, :])
                        elif kind == "qk":
                            if 4 * n + k >= 2:
                                dve.wait_ge(lo_done, at(4 * n + k - 1, 8))
                            take_low(step, at, rest[k % 2][:], src[:], qk_part[0][:, k, :])
                        elif kind == "v":
                            dve.wait_ge(logit_done, at(4 * n + k + 1, 8))
                            nc.vector.tensor_tensor(vaug[n % 2][:, k, :, 0:HD],
                                                    src[:, 0:D].rearrange("p (h j) -> p h j", h=H),
                                                    vb_all[:].rearrange("p (h j) -> p h j", h=H), ALU.add)\
                                .then_inc(shared_done[p], 1)
                        elif kind == "score":
                            u = UN * n + k
                            if u == 0:
                                dve.wait_ge(consts, N_CONST)
                            dve.wait_ge(score_ready, at(u + 1, 8 * UN))
                            if u >= 2:
                                dve.wait_ge(score_done, at(u - 1, 8 * UN))
                            if k == 0 and n >= 2:
                                dve.wait_ge(negmax_done, at(n - 1, 8))
                            dve.sem_inc(dve_past, 1)
                            for h, i, col, width in unit_parts(k, False):
                                last = nc.vector.tensor_tensor_reduce(
                                    out=junk[k % 2][:, col:col + width], in0=SCORE[score_bank(UN * n + k)][:, col:col + width],
                                    in1=rowmask[:, T - width:T], scale=1.0, scalar=-3e38, op0=ALU.add, op1=ALU.max,
                                    accum_out=rowmax[n % 2][:, h, i:i + 1])
                            last.then_inc(score_done, 1)
                            if k == UN - 1:
                                if n >= 2:
                                    prev = ("maxt", n - 2, 0)
                                    dve.wait_ge(shared_ready[bank_of(prev)], filled(prev, at))
                                dve.wait_ge(score_done, at(u + 1, 8 * UN))
                                nc.vector.tensor_scalar(negmax[n % 2][:, 0, :, :], rowmax[n % 2][:], -1.0, None, ALU.mult)\
                                    .then_inc(neghi_done, 1)
                                dve.wait_ge(neghi_done, at(n + 1, 8))
                                nc.vector.scalar_tensor_tensor(out=negmax[n % 2][:, 1, :, :], in0=rowmax[n % 2][:],
                                                               scalar=-1.0, in1=negmax[n % 2][:, 0, :, :],
                                                               op0=ALU.mult, op1=ALU.subtract).then_inc(negmax_done, 1)
                        elif kind == "ytr":
                            dve.wait_ge(shared_ready[p], filled(step, at))
                            y4 = src[:].rearrange("p (q h c) -> p q h c", q=TT, h=GH)
                            if n >= 1:
                                prev = ("ytr", n - 1, 0)
                                dve.wait_ge(shared_done[bank_of(prev)], emptied(prev, at))
                            nc.vector.reciprocal(rden[:], y4[:, :, :, HD]).then_inc(rden_done, 1)
                            dve.wait_ge(rden_done, at(n + 1, 8))
                            if n % GB == 0 and n >= GB:
                                prev = ("yt", n // GB - 1, 1)
                                dve.wait_ge(shared_ready[bank_of(prev)], filled(prev, at))
                            g = n % GB
                            nc.vector.tensor_tensor(
                                ytok[:, :, GH * HD * g:GH * HD * (g + 1)].rearrange("p q (h c) -> p q h c", h=GH),
                                y4[:, :, :, 0:HD], rden[:].unsqueeze(3).to_broadcast([P, TT, GH, HD]), ALU.mult)\
                                .then_inc(shared_done[p], 1)
                        elif kind == "o":
                            dve.wait_ge(shared_ready[p], filled(step, at))
                            dve.wait_ge(xres_done, at(n + 1, 2))
                            nc.vector.tensor_tensor(xres[:, k, :], src[:, 0:D], xres[:, k, :], ALU.add).then_inc(shared_done[p], 1)

                program(dve, steps)

            @block.tensor
            def _(pe):
                pe.wait_ge(ident_done, 1)

                def three_passes(dst, left_hi, left_lo, right_hi, right_lo):
                    todo = [(left(dt), right(dt)) for dt in range(DT)
                            for left, right in ((left_hi, right_hi), (left_hi, right_lo), (left_lo, right_hi))]
                    for m, (a, b) in enumerate(todo):
                        last = nc.tensor.matmul(dst, a, b, start=m == 0, stop=m == len(todo) - 1)
                    return last

                def qk_passes(dst, mt, dt):
                    cols = slice(P * mt, P * mt + P)
                    for m, (a, b) in enumerate(((wqk_hi, xt_hi), (wqk_hi, xt_lo), (wqk_lo, xt_hi))):
                        last = nc.tensor.matmul(dst, a[:, dt, cols], b[:, dt, :],
                                                start=dt == 0 and m == 0, stop=dt == DT - 1 and m == 2)
                    return last

                def await_units(step, sources, at):
                    other = [s for s in sources if bank_of(s) != bank_of(step)] if step in unit_of else sources
                    for u in range(2):
                        mine = [s for s in other if bank_of(s) == u]
                        if mine:
                            pe.wait_ge(shared_done[u], emptied(max(mine, key=unit_of.get), at))

                def steps(todo, at):
                    for step in todo:
                        kind, n, k = step
                        if kind == "qk_first":
                            step = ("qk", n, k)
                        if step in unit_of:
                            p, dst = bank_of(step), SHARED[bank_of(step)]
                            if unit_of[step] >= 2 and kind != "qk":
                                pe.wait_ge(shared_done[p], at(unit_of[step] // 2, U_PAIR // 2))
                        if kind == "rankt":
                            pe.wait_ge(gate_step, 5)
                            for tt in range(TT):
                                last = nc.tensor.transpose(dst[:, P * tt:P * tt + P], gate[:, tt, :], ident[:])
                            last.then_inc(shared_ready[p], 1)
                        elif kind == "rowst":
                            pe.wait_ge(gate_step, GATED + RANK_OPS + 2)
                            nc.tensor.transpose(dst[:, 0:P], top_row, ident[:])
                            nc.tensor.transpose(dst[:, P:2 * P], top, ident[:]).then_inc(shared_ready[p], 1)
                        elif kind == "foldt":
                            pe.wait_ge(fold_a_in[n], 16)
                            w, dt = divmod(n, DT)
                            for c in range(4):
                                h = 2 * (4 * k + c)
                                last = nc.tensor.transpose(dst[:, P * c:P * c + P],
                                                           fold_raw[w][:, dt, h:h + 2, :].rearrange("p h r -> p (h r)"), ident[:])
                            last.then_inc(shared_ready[p], 1)
                        elif kind == "fold":
                            if n % DT == 0:
                                pe.wait_ge(fold_b_in[n // DT], 16 * 2)
                            await_units(step, [("foldt", n, half) for half in range(2)], at)
                            for c in range(H // 2):
                                last = nc.tensor.matmul(dst[:, 2 * HD * c:2 * HD * c + 2 * HD],
                                                        fold_t[n][c // 4][:, P * (c % 4):P * (c % 4) + P],
                                                        foldb[:, n // DT, c, :], start=True, stop=True)
                            last.then_inc(shared_ready[p], 1)
                        elif kind == "wv":
                            pe.wait_ge(weights_in, N_WEIGHTS)
                            for t in range(DT):
                                nc.tensor.transpose(dst[:, P * t:P * t + P], vw_raw[:, t, P * n:P * n + P], ident[:])
                            nc.tensor.transpose(dst[:, D:D + E], choice_raw[:, P * n:P * n + P], ident[0:E, 0:E])\
                                .then_inc(shared_ready[p], 1)
                        elif kind == "wo":
                            pe.wait_ge(out_weights_in, N_OUT_WEIGHTS)
                            for t in range(DT):
                                last = nc.tensor.transpose(dst[:, P * t:P * t + P], ow_raw[:, t, P * n:P * n + P], ident[:])
                            last.then_inc(shared_ready[p], 1)
                        elif kind == "xt":
                            pe.wait_ge(xn_done, at(n + 1, 2))
                            for tt in range(TT):
                                last = nc.tensor.transpose(dst[:, P * tt:P * tt + P], xn[:, tt, P * k:P * k + P], ident[:])
                            last.then_inc(shared_ready[p], 1)
                        elif kind == "qk_first":
                            await_units(step, [("xt", n, dt) for dt in range(DT)]
                                        + [("fold", DT * (k // 2) + dt, 0) for dt in range(DT) if n == 0], at)
                            qk_passes(dst[:], k, 0)
                        elif kind == "qk":
                            qk_passes(dst[:], k, 1).then_inc(shared_ready[p], 1)
                        elif kind == "v":
                            await_units(step, [("wv", dt, 0) for dt in range(DT) if n == 0], at)
                            rows = slice(P * k, P * k + P)
                            three_passes(dst[:, 0:D + E], lambda dt: xt_hi[:, dt, rows], lambda dt: xt_lo[:, dt, rows],
                                         lambda dt: wv_hi[:, dt, :], lambda dt: wv_lo[:, dt, :]).then_inc(shared_ready[p], 1)
                        elif kind == "score":
                            u, (b, g) = UN * n + k, divmod(n, GB)
                            if u >= 3:
                                pe.wait_ge(score_done, at(u - score_back(u) + 1, 8 * UN))
                            if g == 0 and k == 0:
                                pe.wait_ge(stacked[b % 2], at(STACK_DMAS * (b // 2 + 1), STACK_DMAS))
                            for h, i, col, width in unit_parts(k, False):
                                last = nc.tensor.matmul(SCORE[score_bank(UN * n + k)][:, col:col + width],
                                                        qstk[b % 2][0:KS, GH * g + h, P * i:P * i + P],
                                                        kstk[b % 2][0:KS, GH * g + h, 0:width], start=True, stop=True)
                            last.then_inc(score_ready, 1)
                        elif kind == "maxt":
                            pe.wait_ge(negmax_done, at(n + 1, 8))
                            if n == 0:
                                pe.wait_ge(consts, N_CONST)
                            nc.tensor.transpose(dst[:].bitcast(bf16)[0:SHIFT * GH * TT, 0:P],
                                                negmax[n % 2][:].rearrange("p s h i -> p (s h i)"), ident_bf[:])\
                                .then_inc(shared_ready[p], 1)
                        elif kind == "scoret":
                            u, (b, g) = UN * n + k, divmod(n, GB)
                            if u >= 2:
                                pe.wait_ge(exp_done, at(u - 1, 8 * UN))
                            if u == 0:
                                pe.wait_ge(ones_in, 16 * 2)
                            if k == 0:
                                pe.wait_ge(max_in[n % 2], at(32 * (n // 2 + 1), 128))
                            for h, j, col, width in unit_parts(k, True):
                                nc.tensor.matmul(SCORET[k % 2][:, col:col + width],
                                                 kstk[b % 2][0:KS + SHIFT, GH * g + h, P * j:P * j + P],
                                                 qstk[b % 2][0:KS + SHIFT, GH * g + h, P * j:T], start=True, stop=False)
                                last = nc.tensor.matmul(SCORET[k % 2][:, col:col + P], colmask[:], ident_bf[:],
                                                        start=False, stop=True)
                            last.then_inc(scoret_ready, 1)
                        elif kind == "pv":
                            b, g = divmod(n, GB)
                            if k == 0:
                                pe.wait_ge(exp_done, at(UN * (n + 1), 8 * UN))
                                if n == 0:
                                    pe.wait_ge(ones_done, 3)
                                if g == 0:
                                    await_units(step, [("v", b, tt) for tt in range(TT)], at)
                                if n >= 1:
                                    pe.wait_ge(yraw_done, at(n, 8))
                            where = {(h, j): (512 * t + col, width) for t in range(UN)
                                     for h, j, col, width in unit_parts(t, True)}
                            for h in range(GH):
                                col, width = where[h, k]
                                last = nc.tensor.matmul(Y[2 * HD * h:2 * HD * h + 2 * HD, P * k:T],
                                                        vaug[b % 2][:, k, GH * g + h, :],
                                                        probs[n % 2][:, col:col + width],
                                                        start=k == 0, stop=k == TT - 1)
                            if k == TT - 1:
                                last.then_inc(pv_ready, 1)
                        elif kind == "ytr":
                            pe.wait_ge(yraw_done, at(n + 1, 8))
                            for i in range(TT):
                                last = nc.tensor.transpose(dst[:, P * i:P * i + P], yraw[n % 2][:, P * i:P * i + P], ident[:])
                            last.then_inc(shared_ready[p], 1)
                        elif kind == "yt":
                            await_units(step, [("ytr", GB * n + g, 0) for g in range(GB)], at)
                            for tt in range(TT):
                                last = nc.tensor.transpose(dst[:, P * tt:P * tt + P], ytok[:, tt, P * k:P * k + P], ident[:])
                            last.then_inc(shared_ready[p], 1)
                        elif kind == "o":
                            await_units(step, [("yt", n, dt) for dt in range(DT)]
                                        + [("wo", dt, 0) for dt in range(DT) if n == 0], at)
                            rows = slice(P * k, P * k + P)
                            three_passes(dst[:, 0:D], lambda dt: yt_hi[:, dt, rows], lambda dt: yt_lo[:, dt, rows],
                                         lambda dt: wo_hi[:, dt, :], lambda dt: wo_lo[:, dt, :]).then_inc(shared_ready[p], 1)

                program(pe, steps)

        experts(nc, sem, ident, banks, moe, xn_dram, out_rows)


def expert_steps(e):
    out = []
    for grp in range(EG):
        n = EG * e + grp
        out += [("h", n, ft) for ft in range(FT)]
        if grp == EG - 1 and e + 1 < E:
            out += [("w", e + 1, 0), ("w_low", e + 1, 0)]
        if n + 1 < E * EG:
            out += [("pick", n + 1, dt) for dt in range(DT)]
        if n + 2 < E * EG:
            out.append(("gather", n + 2, 0))
        if n >= 1:
            out += [("down", n - 1, j) for j in range(GB4 // 2)]
        if grp == 0 and e >= 1:
            out += [("w", e, 1), ("w_low", e, 1)]
    return out + [("down", n, j) for j in range(GB4 // 2) if e == E - 1]


def gather(nc, moe, xn_dram, n):
    grp = n % EG
    for j in range(GB4):
        nc.gpsimd.indirect_dma_start(
            out=moe.picked[n % 2][:, j, :], out_offset=None, in_=xn_dram,
            in_offset=bass.IndirectOffsetOnAxis(ap=moe.row_sel[grp][:, j, :], axis=0)).then_inc(moe.gathered[grp], 16)


def select(nc, moe, n, e):
    grp = n % EG
    of = slice(GB4 * grp, GB4 * grp + GB4)
    nc.vector.tensor_copy(moe.gate_sel[grp][:], moe.gates[:, of, bass.ds(e, 1)])
    nc.vector.tensor_copy(moe.row_sel[grp][:], moe.rows[:, of, bass.ds(e, 1)]).then_inc(moe.sel_done, 1)


def experts(nc, sem, ident, banks, moe, xn_dram, out_rows):
    fp32, f32r = mybir.dt.float32, mybir.dt.float32r
    ALU, ACT = mybir.AluOpType, mybir.ActivationFunctionType
    assert B * E == P and CAP == P
    start_steps = [("gather", 1, 0), ("w", 0, 0), ("pick", 0, 0), ("pick", 0, 1), ("w_low", 0, 0), ("w", 0, 1),
                   ("w_low", 0, 1)]
    row_sel, gate_sel, picked, gathered, sel_done = moe.row_sel, moe.gate_sel, moe.picked, moe.gathered, moe.sel_done
    with ExitStack() as mem:
        def sb(name, shape, dt):
            return mem.enter_context(nc.sbuf_tensor(name, shape, dt))

        w_hi = [sb(f"w{w}_hi", [P, DT * F], f32r) for w in (1, 2)]
        w_lo = [sb(f"w{w}_lo", [P, DT * F], f32r) for w in (1, 2)]
        w1_hi, w1_lo = (t[0][:].rearrange("p (t f) -> p t f", t=DT) for t in (w_hi, w_lo))
        w2_hi, w2_lo = (t[1][:].rearrange("p (t d) -> p t d", t=FT) for t in (w_hi, w_lo))
        pt_hi, pt_lo = sb("pt_hi", [P, DT, T], f32r), sb("pt_lo", [P, DT, T], f32r)
        hid = [sb(f"hid{u}", [P, T], fp32) for u in range(2)]
        hid_hi = [sb(f"hid_hi{u}", [P, FT, T], f32r) for u in range(2)]
        hid_lo = [sb(f"hid_lo{u}", [P, FT, T], f32r) for u in range(2)]
        mixed = [sb(f"mixed{u}", [P, GB4, D], fp32) for u in range(2)]
        PICK, UP, DOWN = banks[0:2], banks[2:6], banks[6:8]

        pool_past, sp_past = sem("pool_past2"), sem("sp_past2")
        w_in = moe.w_in
        w_high = [sem(f"w{w}_high") for w in (1, 2)]
        w_done = [sem(f"w{w}_done") for w in (1, 2)]
        pick_ready, pick_hi, pick_done = sem("pick_ready"), sem("pick_hi"), sem("pick_done")
        up_ready, silu_done, hid_high, hid_done = sem("up_ready"), sem("silu_done"), sem("hid_high"), sem("hid_done")
        down_ready, mixed_done = sem("down_ready"), sem("mixed_done")
        added = [sem(f"added{g}") for g in range(EG)]

        def program(eng, steps_fn):
            same = lambda value, per_expert: value
            steps_fn(start_steps + expert_steps(0), same)
            with eng.Fori(1, E - 1) as e:
                steps_fn(expert_steps(1), lambda value, per_expert: e * per_expert + (value - per_expert))
            steps_fn(expert_steps(E - 1), same)

        block = mem.enter_context(nc.Block())

        @block.sync
        def _(sp):
            def steps(todo, at):
                for kind, n, k in todo:
                    sp.wait_ge(w_done[k], at(n, 1))
                    sp.sem_inc(sp_past, 1)
                    sp.dma_start(moe.w_raw[k], moe.w_view[k][at(n, 1)]).then_inc(w_in[k], 16)

            def ahead(todo, at):
                steps([(kind, n, k) for kind, n, k in todo if kind == "w" and n >= 1], at)

            program(sp, ahead)

        @block.gpsimd
        def _(pool):
            def steps(todo, at):
                for kind, n, k in todo:
                    grp = n % EG
                    if kind == "gather":
                        pool.wait_ge(sel_done, at(n + 1, EG))
                        if n >= 2:
                            pool.wait_ge(pick_ready, at(DT * (n - 1), EG * DT))
                        pool.sem_inc(pool_past, 1)
                        gather(nc, moe, xn_dram, n)
                    elif kind == "down":
                        pool.wait_ge(mixed_done, at(GB4 // 2 * n + k + 1, EG * GB4 // 2))
                        if n == 0 and k == 0:
                            pool.wait_ge(moe.out_stored, 16 * B)
                        if n >= EG and k == 0:
                            pool.wait_ge(added[grp], at(16 * GB4 * (n // EG), 16 * GB4))
                        pool.sem_inc(pool_past, 1)
                        for j in (2 * k, 2 * k + 1):
                            nc.gpsimd.indirect_dma_start(
                                out=out_rows, out_offset=bass.IndirectOffsetOnAxis(ap=row_sel[grp][:, j, :], axis=0),
                                in_=mixed[n % 2][:, j, :], in_offset=None, compute_op=ALU.add).then_inc(added[grp], 16)

            program(pool, steps)
            for g in range(EG):
                pool.wait_ge(added[g], 16 * GB4 * E)

        @block.scalar
        def _(act):
            def steps(todo, at):
                for kind, n, k in todo:
                    if kind == "w":
                        act.wait_ge(w_in[k], at(16 * (n + 1), 16))
                        if k == 0 and n >= 1:
                            act.wait_ge(up_ready, at(FT * EG * n, FT * EG))
                        elif n >= 1:
                            act.wait_ge(down_ready, at(GB4 // 2 * EG * n, GB4 // 2 * EG))
                        nc.scalar.activation(w_hi[k][:], moe.w_raw[k], ACT.Copy).then_inc(w_high[k], 1)
                    elif kind == "pick":
                        act.wait_ge(pick_ready, at(DT * n + k + 1, DT * EG))
                        nc.scalar.activation(pt_hi[:, k, :], PICK[k][:], ACT.Copy).then_inc(pick_hi, 1)
                    elif kind == "h":
                        act.wait_ge(up_ready, at(FT * n + k + 1, FT * EG))
                        if FT * n + k >= 2:
                            act.wait_ge(hid_done, at(FT * n + k - 1, FT * EG))
                        nc.scalar.activation(hid[k % 2][:], UP[k][:], ACT.Silu).then_inc(silu_done, 1)

            program(act, steps)

        @block.vector
        def _(dve):
            def steps(todo, at):
                for kind, n, k in todo:
                    grp = n % EG
                    if kind == "w_low":
                        dve.wait_ge(w_high[k], at(n + 1, 1))
                        nc.vector.tensor_tensor(w_lo[k][:], moe.w_raw[k], w_hi[k][:], ALU.subtract).then_inc(w_done[k], 1)
                    elif kind == "gather":
                        if n >= EG:
                            dve.wait_ge(added[grp], at(16 * GB4 * (n // EG), 16 * GB4))
                        select(nc, moe, n, at(n // EG, 1))
                    elif kind == "pick":
                        dve.wait_ge(pick_hi, at(DT * n + k + 1, DT * EG))
                        nc.vector.tensor_tensor(pt_lo[:, k, :], PICK[k][:], pt_hi[:, k, :], ALU.subtract).then_inc(pick_done, 1)
                    elif kind == "h":
                        u = FT * n + k
                        dve.wait_ge(silu_done, at(u + 1, FT * EG))
                        nc.vector.tensor_copy(hid_hi[n % 2][:, k, :], hid[k % 2][:]).then_inc(hid_high, 1)
                        dve.wait_ge(hid_high, at(u + 1, FT * EG))
                        nc.vector.tensor_tensor(hid_lo[n % 2][:, k, :], hid[k % 2][:], hid_hi[n % 2][:, k, :], ALU.subtract).then_inc(hid_done, 1)
                    elif kind == "down":
                        u = GB4 // 2 * n + k
                        dve.wait_ge(down_ready, at(u + 1, GB4 // 2 * EG))
                        dve.wait_ge(sel_done, at(n + 1, EG))
                        if n >= 2 and k == 0:
                            dve.wait_ge(added[(n - 2) % EG], at(16 * GB4 * ((n - 2) // EG + 1), 16 * GB4))
                        for t in range(2):
                            j = 2 * k + t
                            last = nc.vector.tensor_scalar(mixed[n % 2][:, j, :], DOWN[k][:, D * t:D * t + D],
                                                           gate_sel[grp][:, j, :], None, ALU.mult)
                        last.then_inc(mixed_done, 1)

            program(dve, steps)

        @block.tensor
        def _(pe):
            def steps(todo, at):
                for kind, n, k in todo:
                    if kind == "pick":
                        if k == 0:
                            pe.wait_ge(gathered[n % EG], at(16 * GB4 * (n // EG + 1), 16 * GB4))
                        if n >= 1:
                            pe.wait_ge(pick_done, at(DT * (n - 1) + k + 1, DT * EG))
                        for j in range(GB4):
                            last = nc.tensor.transpose(PICK[k][:, P * j:P * j + P], picked[n % 2][:, j, P * k:P * k + P], ident[:])
                        last.then_inc(pick_ready, 1)
                    elif kind == "h":
                        u = FT * n + k
                        if k == 0:
                            pe.wait_ge(pick_done, at(DT * (n + 1), DT * EG))
                            if n == 0:
                                pe.wait_ge(w_high[0], 1)
                        if n >= 1:
                            pe.wait_ge(silu_done, at(u - FT + 1, FT * EG))
                        f = slice(P * k, P * k + P)
                        passes = ((w1_hi, pt_hi), (w1_hi, pt_lo), (w1_lo, pt_hi))
                        for m, (a, b) in enumerate(passes):
                            if k == 0 and m == 2 and n % EG == 0:
                                pe.wait_ge(w_done[0], at(n // EG + 1, 1))
                            for dt in range(DT):
                                last = nc.tensor.matmul(UP[k][:], a[:, dt, f], b[:, dt, :],
                                                        start=m == 0 and dt == 0, stop=m == 2 and dt == DT - 1)
                        last.then_inc(up_ready, 1)
                    elif kind == "down":
                        u = GB4 // 2 * n + k
                        if k == 0:
                            pe.wait_ge(hid_done, at(FT * (n + 1), FT * EG))
                            if n % EG == 0:
                                pe.wait_ge(w_done[1], at(n // EG + 1, 1))
                        if n >= 1:
                            pe.wait_ge(mixed_done, at(u - 1, GB4 // 2 * EG))
                        for t in range(2):
                            r = slice(P * (2 * k + t), P * (2 * k + t) + P)
                            todo_mm = [(a[:, ft, r], b[:, ft, :]) for ft in range(FT)
                                       for a, b in ((hid_hi[n % 2], w2_hi), (hid_hi[n % 2], w2_lo), (hid_lo[n % 2], w2_hi))]
                            for m, (a, b) in enumerate(todo_mm):
                                last = nc.tensor.matmul(DOWN[k][:, D * t:D * t + D], a, b, start=m == 0, stop=m == len(todo_mm) - 1)
                        last.then_inc(down_ready, 1)

            program(pe, steps)


_INS = ["L0_attn_hidden_states", "L0_attn_q_a", "L0_attn_q_b", "L0_attn_k_a", "L0_attn_k_b", "L0_attn_v_w",
        "L0_attn_v_b", "L0_attn_o_w", "L0_attn_o_b", "L0_ffn_choice_w", "L0_ffn_w1", "L0_ffn_w2"]


def kernel(**inputs):
    import numpy as np
    import concourse.bacc as bacc
    from concourse.bass_utils import run_bass_kernel_spmd

    nc = bacc.Bacc("TRN2", target_bir_lowering=False, num_devices=1)
    arrays, args = {}, []
    for name in _INS:
        a = np.ascontiguousarray(inputs[name])
        arrays[f"in_{name}"] = a
        args.append(nc.dram_tensor(f"in_{name}", a.shape, mybir.dt.from_np(a.dtype), kind="ExternalInput").ap())
    out = nc.dram_tensor("out_rows", (B, T, D), mybir.dt.float32, kind="ExternalOutput").ap()
    build(nc, *args, out)
    r = run_bass_kernel_spmd(nc, [arrays], core_ids=[0])
    return r.results[0]["out_rows"]
```
